# Optimizing a Trainium2 kernel written in Bass

```python
import numpy as np
import jax
import jax.numpy as jnp

def _softmax(x, axis=-1):
    return jax.nn.softmax(x, axis=axis)
def _gelu(x):
    return jax.nn.gelu(x, approximate=True)
def _silu(x):
    return jax.nn.silu(x)
def _sigmoid(x):
    return jax.nn.sigmoid(x)
def _layernorm(x, axis=-1, eps=1e-5):
    m = jnp.mean(x, axis=axis, keepdims=True)
    v = jnp.var(x, axis=axis, keepdims=True)
    return (x - m) / jnp.sqrt(v + eps)
def _scatter_add(tgt, idx, src, axis=0):
    return tgt.at[idx].add(src)
def _segment_sum(src, seg, n):
    return jax.ops.segment_sum(src, seg, n)

kernel_name = 'mk_conv_seq_d2_conv_nchw64_1021e3'

def setup_inputs(seed: int = 0):
    np.random.seed(seed)
    _w = jnp.asarray
    def _rec_inputs():
        import jax
        import jax.numpy as jnp
        _gk = jax.random.key(seed)
        x = -0.0002928 + 1 * jax.random.normal(jax.random.fold_in(_gk, 1), (16, 64, 64, 64), jnp.float32)
        return x
    x = _rec_inputs()
    def _L0_conv_setup():
        import jax, jax.numpy as jnp
        import numpy as np
        B, C, H, W = (16, 64, 64, 64)
        EXPAND, D_CONV, D_STATE = (2, 4, 16)
        D_INNER = EXPAND * C
        DT_RANK = (C + 15) // 16
        LEAK = 0.01

        def leaky_relu(x):
            return jnp.where(x >= 0, x, LEAK * x)

        def conv2d_3x3(x, w, b):
            y = jax.lax.conv_general_dilated(x, w, (1, 1), ((1, 1), (1, 1)), dimension_numbers=('NCHW', 'OIHW', 'NCHW'))
            return y + b[None, :, None, None]

        def mamba(xseq, in_proj_w, conv1d_w, conv1d_b, x_proj_w, dt_proj_w, dt_proj_b, A_log, D, out_proj_w):
            bN, L, _ = xseq.shape
            xz = xseq @ in_proj_w
            x, z = jnp.split(xz, 2, axis=-1)
            k = conv1d_w.shape[-1]
            xc = jnp.transpose(x, (0, 2, 1))
            xc = jnp.pad(xc, ((0, 0), (0, 0), (k - 1, 0)))
            xc = jax.lax.conv_general_dilated(xc, conv1d_w, (1,), 'VALID', dimension_numbers=('NCH', 'OIH', 'NCH'), feature_group_count=D_INNER)
            x = jax.nn.silu(jnp.transpose(xc + conv1d_b[None, :, None], (0, 2, 1)))
            dbc = x @ x_proj_w
            dt = dbc[..., :DT_RANK]
            Bm = dbc[..., DT_RANK:DT_RANK + D_STATE]
            Cm = dbc[..., DT_RANK + D_STATE:]
            delta = jax.nn.softplus(dt @ dt_proj_w + dt_proj_b)
            A = -jnp.exp(A_log)

            def step(h, inp):
                d_t, u_t, b_t, c_t = inp
                h = jnp.exp(d_t[..., None] * A) * h + (d_t * u_t)[..., None] * b_t[:, None, :]
                y = jnp.einsum('bdn,bn->bd', h, c_t)
                return (h, y)
            h0 = jnp.zeros((bN, D_INNER, D_STATE), xseq.dtype)
            xs = (jnp.moveaxis(delta, 1, 0), jnp.moveaxis(x, 1, 0), jnp.moveaxis(Bm, 1, 0), jnp.moveaxis(Cm, 1, 0))
            _, ys = jax.lax.scan(step, h0, xs)
            y = jnp.moveaxis(ys, 0, 1) + x * D
            y = y * jax.nn.silu(z)
            return y @ out_proj_w
        key = jax.random.key(seed)
        ks = jax.random.split(key, 14)
        s = 0.02
        inp = {'x': jax.random.normal(ks[0], (B, C, H, W), jnp.float32), 'conv_w1': jax.random.normal(ks[1], (C, C, 3, 3), jnp.float32) * s, 'conv_b1': jnp.zeros((C,), jnp.float32), 'conv_w2': jax.random.normal(ks[2], (C, C, 3, 3), jnp.float32) * s, 'conv_b2': jnp.zeros((C,), jnp.float32), 'in_proj_w': jax.random.normal(ks[3], (C, 2 * D_INNER), jnp.float32) * s, 'conv1d_w': jax.random.normal(ks[4], (D_INNER, 1, D_CONV), jnp.float32) * s, 'conv1d_b': jnp.zeros((D_INNER,), jnp.float32), 'x_proj_w': jax.random.normal(ks[5], (D_INNER, DT_RANK + 2 * D_STATE), jnp.float32) * s, 'dt_proj_w': jax.random.normal(ks[6], (DT_RANK, D_INNER), jnp.float32) * s, 'dt_proj_b': jnp.full((D_INNER,), -4.0, jnp.float32), 'A_log': jnp.log(jnp.tile(jnp.arange(1, D_STATE + 1, dtype=jnp.float32), (D_INNER, 1))), 'D': jnp.ones((D_INNER,), jnp.float32), 'out_proj_w': jax.random.normal(ks[7], (D_INNER, C), jnp.float32) * s}
        return inp
    _L0_conv_all = _L0_conv_setup()
    _L0_conv_in = {k: v for k, v in _L0_conv_all.items() if k in ('conv_w1', 'conv_b1', 'conv_w2', 'conv_b2', 'in_proj_w', 'conv1d_w', 'conv1d_b', 'x_proj_w', 'dt_proj_w', 'dt_proj_b', 'A_log', 'D', 'out_proj_w', )}
    del _L0_conv_all

    def _L1_conv_setup():
        import jax, jax.numpy as jnp
        import numpy as np
        C, H, W, B = (64, 64, 64, 8)

        def _conv1x1(w, x):
            return jnp.einsum('oc,bchw->bohw', w, x)
        key = jax.random.key(seed)
        ks = jax.random.split(key, 6)
        s = 0.05
        return {'x': jax.random.normal(ks[0], (B, C, H, W), dtype=jnp.float32), 'w_cam': jax.random.normal(ks[1], (C, C), dtype=jnp.float32) * s, 'w_q': jax.random.normal(ks[2], (C // 2, C), dtype=jnp.float32) * s, 'w_k': jax.random.normal(ks[3], (C // 2, C), dtype=jnp.float32) * s, 'w_v': jax.random.normal(ks[4], (C, C), dtype=jnp.float32) * s, 'w_bn': jax.random.normal(ks[5], (C, 2 * C), dtype=jnp.float32) * s}
    _L1_conv_all = _L1_conv_setup()
    _L1_conv_in = {k: v for k, v in _L1_conv_all.items() if k in ('w_cam', 'w_q', 'w_k', 'w_v', 'w_bn', )}
    del _L1_conv_all

    return {
        "x": x,
        "L0_conv_conv_w1": _L0_conv_in["conv_w1"],
        "L0_conv_conv_b1": _L0_conv_in["conv_b1"],
        "L0_conv_conv_w2": _L0_conv_in["conv_w2"],
        "L0_conv_conv_b2": _L0_conv_in["conv_b2"],
        "L0_conv_in_proj_w": _L0_conv_in["in_proj_w"],
        "L0_conv_conv1d_w": _L0_conv_in["conv1d_w"],
        "L0_conv_conv1d_b": _L0_conv_in["conv1d_b"],
        "L0_conv_x_proj_w": _L0_conv_in["x_proj_w"],
        "L0_conv_dt_proj_w": _L0_conv_in["dt_proj_w"],
        "L0_conv_dt_proj_b": _L0_conv_in["dt_proj_b"],
        "L0_conv_A_log": _L0_conv_in["A_log"],
        "L0_conv_D": _L0_conv_in["D"],
        "L0_conv_out_proj_w": _L0_conv_in["out_proj_w"],
        "L1_conv_w_cam": _L1_conv_in["w_cam"],
        "L1_conv_w_q": _L1_conv_in["w_q"],
        "L1_conv_w_k": _L1_conv_in["w_k"],
        "L1_conv_w_v": _L1_conv_in["w_v"],
        "L1_conv_w_bn": _L1_conv_in["w_bn"],
    }

def reference(x, L0_conv_conv_w1, L0_conv_conv_b1, L0_conv_conv_w2, L0_conv_conv_b2, L0_conv_in_proj_w, L0_conv_conv1d_w, L0_conv_conv1d_b, L0_conv_x_proj_w, L0_conv_dt_proj_w, L0_conv_dt_proj_b, L0_conv_A_log, L0_conv_D, L0_conv_out_proj_w, L1_conv_w_cam, L1_conv_w_q, L1_conv_w_k, L1_conv_w_v, L1_conv_w_bn):
    import jax
    import jax.numpy as jnp
    def _L0_conv_ref(x, conv_w1, conv_b1, conv_w2, conv_b2, in_proj_w, conv1d_w, conv1d_b, x_proj_w, dt_proj_w, dt_proj_b, A_log, D, out_proj_w):
        import jax, jax.numpy as jnp
        import numpy as np
        B, C, H, W = (16, 64, 64, 64)
        EXPAND, D_CONV, D_STATE = (2, 4, 16)
        D_INNER = EXPAND * C
        DT_RANK = (C + 15) // 16
        LEAK = 0.01

        def leaky_relu(x):
            return jnp.where(x >= 0, x, LEAK * x)

        def conv2d_3x3(x, w, b):
            y = jax.lax.conv_general_dilated(x, w, (1, 1), ((1, 1), (1, 1)), dimension_numbers=('NCHW', 'OIHW', 'NCHW'))
            return y + b[None, :, None, None]

        def mamba(xseq, in_proj_w, conv1d_w, conv1d_b, x_proj_w, dt_proj_w, dt_proj_b, A_log, D, out_proj_w):
            bN, L, _ = xseq.shape
            xz = xseq @ in_proj_w
            x, z = jnp.split(xz, 2, axis=-1)
            k = conv1d_w.shape[-1]
            xc = jnp.transpose(x, (0, 2, 1))
            xc = jnp.pad(xc, ((0, 0), (0, 0), (k - 1, 0)))
            xc = jax.lax.conv_general_dilated(xc, conv1d_w, (1,), 'VALID', dimension_numbers=('NCH', 'OIH', 'NCH'), feature_group_count=D_INNER)
            x = jax.nn.silu(jnp.transpose(xc + conv1d_b[None, :, None], (0, 2, 1)))
            dbc = x @ x_proj_w
            dt = dbc[..., :DT_RANK]
            Bm = dbc[..., DT_RANK:DT_RANK + D_STATE]
            Cm = dbc[..., DT_RANK + D_STATE:]
            delta = jax.nn.softplus(dt @ dt_proj_w + dt_proj_b)
            A = -jnp.exp(A_log)

            def step(h, inp):
                d_t, u_t, b_t, c_t = inp
                h = jnp.exp(d_t[..., None] * A) * h + (d_t * u_t)[..., None] * b_t[:, None, :]
                y = jnp.einsum('bdn,bn->bd', h, c_t)
                return (h, y)
            h0 = jnp.zeros((bN, D_INNER, D_STATE), xseq.dtype)
            xs = (jnp.moveaxis(delta, 1, 0), jnp.moveaxis(x, 1, 0), jnp.moveaxis(Bm, 1, 0), jnp.moveaxis(Cm, 1, 0))
            _, ys = jax.lax.scan(step, h0, xs)
            y = jnp.moveaxis(ys, 0, 1) + x * D
            y = y * jax.nn.silu(z)
            return y @ out_proj_w
        bN, cN, hN, wN = x.shape
        y = leaky_relu(conv2d_3x3(x, conv_w1, conv_b1))
        y = leaky_relu(conv2d_3x3(y, conv_w2, conv_b2))
        seq = y.reshape(bN, cN, hN * wN).transpose(0, 2, 1)
        seq = mamba(seq, in_proj_w, conv1d_w, conv1d_b, x_proj_w, dt_proj_w, dt_proj_b, A_log, D, out_proj_w)
        return seq.transpose(0, 2, 1).reshape(bN, cN, hN, wN)

    def _L1_conv_ref(x, w_cam, w_q, w_k, w_v, w_bn):
        import jax, jax.numpy as jnp
        import numpy as np
        C, H, W, B = (64, 64, 64, 8)

        def _conv1x1(w, x):
            return jnp.einsum('oc,bchw->bohw', w, x)
        b, c, h, w = x.shape
        hw = h * w
        xc = _conv1x1(w_cam, x).reshape(b, c, hw)
        energy_c = jnp.einsum('bcn,bdn->bcd', xc, xc)
        attn_c = jax.nn.softmax(energy_c, axis=-1)
        out_c = jnp.einsum('bcd,bdn->bcn', attn_c, x.reshape(b, c, hw)).reshape(b, c, h, w)
        q = _conv1x1(w_q, x).reshape(b, c // 2, hw)
        k = _conv1x1(w_k, x).reshape(b, c // 2, hw)
        v = _conv1x1(w_v, x).reshape(b, c, hw)
        energy_s = jnp.einsum('bcn,bcm->bnm', q, k)
        attn_s = jax.nn.softmax(energy_s, axis=-1)
        out_s = jnp.einsum('bcm,bnm->bcn', v, attn_s).reshape(b, c, h, w)
        cat = jnp.concatenate([out_c, out_s], axis=1)
        out = _conv1x1(w_bn, cat)
        return x + out

    def _gn(v, G=32, eps=1e-5):
        B_, C_, H_, W_ = v.shape
        g = v.reshape(B_, G, C_ // G, H_, W_)
        m = jnp.mean(g, axis=(2, 3, 4), keepdims=True)
        s = jnp.var(g, axis=(2, 3, 4), keepdims=True)
        return ((g - m) / jnp.sqrt(s + eps)).reshape(v.shape)

    def _ln_c(v, eps=1e-6):
        m = jnp.mean(v, axis=1, keepdims=True)
        s = jnp.var(v, axis=1, keepdims=True)
        return (v - m) / jnp.sqrt(s + eps)

    def _ln_t(v, eps=1e-5):
        m = jnp.mean(v, axis=-1, keepdims=True)
        s = jnp.var(v, axis=-1, keepdims=True)
        return (v - m) / jnp.sqrt(s + eps)

    def _to_tokens(v):
        B_, C_, H_, W_ = v.shape
        return v.reshape(B_, C_, H_ * W_).transpose(0, 2, 1)
    def _from_tokens(t, like):
        B_, C_, H_, W_ = like.shape
        return t.transpose(0, 2, 1).reshape(B_, C_, H_, W_)

    x = _L0_conv_ref(x, L0_conv_conv_w1, L0_conv_conv_b1, L0_conv_conv_w2, L0_conv_conv_b2, L0_conv_in_proj_w, L0_conv_conv1d_w, L0_conv_conv1d_b, L0_conv_x_proj_w, L0_conv_dt_proj_w, L0_conv_dt_proj_b, L0_conv_A_log, L0_conv_D, L0_conv_out_proj_w)
    x = _L1_conv_ref(x, L1_conv_w_cam, L1_conv_w_q, L1_conv_w_k, L1_conv_w_v, L1_conv_w_bn)
    return x


_drawn_inputs = setup_inputs


def setup_inputs(seed=0):
    import zlib

    import numpy as np

    out = dict(_drawn_inputs(seed))
    spreads = {'L0_conv_conv_b1': (0.0, 0.1),
     'L0_conv_conv_b2': (0.0, 0.1),
     'L0_conv_conv1d_b': (0.0, 0.1),
     'L0_conv_dt_proj_b': (-4.0, 0.6),
     'L0_conv_D': (1.0, 0.2)}
    factors = {'L0_conv_conv1d_w': 6.263,
     'L0_conv_x_proj_w': 64.0,
     'L0_conv_dt_proj_w': 64.0,
     'L0_conv_A_log': 64.0,
     'L1_conv_w_cam': 64.0,
     'L1_conv_w_q': 64.0,
     'L1_conv_w_k': 64.0}
    for name, (base, spread) in spreads.items():
        noise = np.random.default_rng([zlib.crc32(name.encode()), seed]).standard_normal(out[name].shape)
        drawn = base * np.exp(spread * noise) if base else spread * noise
        out[name] = jnp.asarray(drawn.astype(out[name].dtype))
    for name, factor in factors.items():
        out[name] = (out[name] * factor).astype(out[name].dtype)
    return out
```

```python
from contextlib import ExitStack

import concourse.bass as bass
from concourse import mybir

F32 = mybir.dt.float32
BF16 = mybir.dt.bfloat16
ALU = mybir.AluOpType
ACT = mybir.ActivationFunctionType
AX_X = mybir.AxisListType.X

P = 128
IMAGES, CH, HH, WW = 16, 64, 64, 64
L = HH * WW
PAIRS = IMAGES // 2
PAD = HH + 2
D_INNER, D_STATE, D_CONV, DT_RANK = 128, 16, 4, 4
LEAK = 0.01
A_LOG_MAX = 84.0
CHUNK = 512
CHUNKS = L // CHUNK
ROWS = CHUNK // WW
DL = P // D_STATE
GROUPS = D_INNER // DL
BLOCK = 32
BLOCKS = D_INNER // BLOCK
GPB = BLOCK // DL
QDIM = CH // 2
QUARTER = 1024
QUARTERS = L // QUARTER
KT = L // P
NT = QUARTER // P
TICKS = CHUNKS * GROUPS
assert TICKS == QUARTERS * KT
LEAD, TAIL = GROUPS, 12
PRING = 4
SRING = 4
HRING = 3
MAX_TICKS = KT - 4

C_ID = 0
C_SEL = C_ID + P
C_SUM = C_SEL + GPB * P
C_DEN = C_SUM + GPB * BLOCK
C_MASK = C_DEN + P
C_END = C_MASK + 4


def shape_constants():
    import numpy as np
    c = np.zeros((P, C_END), np.float32)
    c[:, C_ID:C_ID + P] = np.eye(P)
    for lane in range(P):
        for g in range(GPB):
            row = DL * g + lane % DL
            for s in range(3):
                c[BLOCK * s + row, C_SEL + P * g + lane] = 1
            c[lane, C_SUM + BLOCK * g + row] = 1
    for col in range(P):
        half = col // CH
        c[32 * half, C_DEN + col] = 1
        c[64 + 32 * half, C_DEN + col] = 1
    block = np.arange(P) // 32
    c[:, C_MASK] = -1.0 * (block >= 2)
    c[:, C_MASK + 1] = -1.0 * (block % 2 == 1)
    c[:, C_MASK + 2] = -1.0 * (block == 1)
    c[:, C_MASK + 3] = -1.0 * (block == 0)
    return c


def events_of_tick(T, mamba, attn):
    ev = []
    if attn:
        q, t = T // KT + 1, T % KT
        span = MAX_TICKS
        if T < 0:
            q, t, span = 0, T + LEAD, LEAD - 4
        if q < QUARTERS and t < span:
            n = NT * CHUNKS
            ev += [("max", q, k) for k in range(n * t // span, n * (t + 1) // span)]
        if q < QUARTERS and t == span + 1:
            ev.append(("turn", q))
        if T == -LEAD:
            ev.insert(0, ("mix",))
        r = T % KT
        if T >= KT:
            done = T // KT - 1
            ev += [("den", done)] if r == 2 else [("res", done)] if r == 4 else []
    if mamba:
        c, r = T // GROUPS + 1, T % GROUPS
        if c < CHUNKS:
            name = {1: "xin", 2: "z", 6: "dt", 7: "B", 8: "C"}.get(r)
            ev += [(name, c)] if name else []
        c = T // GROUPS - 1
        if c >= 0:
            name = {3: "out", 4: "q", 5: "k", 9: "xv", 10: "en"}.get(r)
            ev += [(name, c)] if name else []
    return ev


def build(nc, x, w1, b1, w2, b2, w_in, cw, cb, w_dt_t, w_dt, dt_b, w_b, w_c, a_log, skip, w_out,
          w_cam_t, w_q4, w_k4, w_v, w_bn1_t, w_bn2_t, consts, out):
    seq_d = nc.dram_tensor("seq_d", [IMAGES, CH, L], F32, kind="Internal").ap()
    x1_d = nc.dram_tensor("x1_d", [CH, L], F32, kind="Internal").ap()
    s1q_d = nc.dram_tensor("s1q_d", [P, L], BF16, kind="Internal").ap()
    t2q_d = nc.dram_tensor("t2q_d", [CH, L], BF16, kind="Internal").ap()
    s1k_d = nc.dram_tensor("s1k_d", [P, L], BF16, kind="Internal").ap()
    t2k_d = nc.dram_tensor("t2k_d", [CH, L], BF16, kind="Internal").ap()
    vt_d = nc.dram_tensor("vt_d", [P, KT, CH], F32, kind="Internal").ap()

    with ExitStack() as top:
        banks = [top.enter_context(nc.psum_tensor(f"bank{i}", [P, 512], F32)) for i in range(8)]
        convolutions(nc, banks, x, w1, b1, w2, b2, seq_d)
        pipeline(nc, banks, seq_d, (x1_d, s1q_d, t2q_d, s1k_d, t2k_d, vt_d), w_in, cw, cb, w_dt_t,
                 w_dt, dt_b, w_b, w_c, a_log, skip, w_out, w_cam_t, w_q4, w_k4, w_v, w_bn1_t,
                 w_bn2_t, consts, out)


def clear(nc, sems):
    for s in sems:
        nc.gpsimd.sem_clear(s)
    nc.all_engine_barrier()


def convolutions(nc, banks, x, w1, b1, w2, b2, seq_d):
    with ExitStack() as ctx:
        def sb(name, shape, dt=F32):
            return ctx.enter_context(nc.sbuf_tensor(name, shape, dt))

        def sem(name):
            return ctx.enter_context(nc.semaphore(name))

        wbd = [sb("w1bd", [P, 9, P]), sb("w2bd", [P, 9, P])]
        bias = sb("bias", [P, 2])
        xpad = sb("xpad", [P, PAD, PAD])
        ypad = sb("ypad", [P, PAD, PAD])
        biased = sb("biased", [P, 2, CHUNK])
        seq = sb("seq", [P, 2, CHUNK])

        zeroed, w_in_sem = sem("zeroed"), sem("conv_weights")
        with nc.Block() as block:
            @block.vector
            def _(dve):
                nc.vector.memset(wbd[0][:], 0.0).then_inc(zeroed, 1)
                nc.vector.memset(wbd[1][:], 0.0).then_inc(zeroed, 1)

            @block.gpsimd
            def _(pool):
                nc.gpsimd.memset(xpad[:], 0.0)
                nc.gpsimd.memset(ypad[:], 0.0)

            @block.sync
            def _(sp):
                sp.wait_ge(zeroed, 2)
                for bd, w, b, col in ((wbd[0], w1, b1, 0), (wbd[1], w2, b2, 1)):
                    for half in (0, CH):
                        sp.dma_start(bd[half:half + CH, :, half:half + CH], w).then_inc(w_in_sem, 16)
                        sp.dma_start(bias[half:half + CH, col:col + 1], b).then_inc(w_in_sem, 16)
                sp.wait_ge(w_in_sem, 8 * 16)
        clear(nc, [zeroed, w_in_sem])

        loaded, summed, plus_bias, leaky = (sem(n) for n in ("loaded", "summed", "plus_bias", "leaky"))
        stored = [sem("stored0"), sem("stored1")]

        def pair(p):
            with nc.Block() as block:
                @block.sync
                def _(sp):
                    src = x[bass.ds(p, 1)].rearrange("a p h w -> (a p) h w")
                    for h in range(4):
                        r = h * 16
                        sp.dma_start(xpad[:, 1 + r:17 + r, 1:1 + WW], src[:, r:r + 16, :]).then_inc(loaded, 16)
                    for k in range(CHUNKS):
                        sp.wait_ge(leaky, CHUNKS + k + 1)
                        sp.dma_start(seq_d[bass.ds(p * 2, 2)].rearrange("a c l -> (a c) l")
                                     [:, k * CHUNK:(k + 1) * CHUNK], seq[:, k % 2, :]).then_inc(stored[k % 2], 16)
                    for s in stored:
                        sp.wait_ge(s, 16 * CHUNKS // 2)

                @block.tensor
                def _(pe):
                    pe.wait_ge(loaded, 64)
                    for n in range(2 * CHUNKS):
                        conv, k = n // CHUNKS, n % CHUNKS
                        src = (xpad, ypad)[conv]
                        if n >= 8:
                            pe.wait_ge(plus_bias, n - 7)
                        if conv:
                            pe.wait_ge(leaky, min(k + 2, CHUNKS))
                        for tap in range(9):
                            dy, dx = tap // 3, tap % 3
                            mm = nc.tensor.matmul(
                                banks[n % 8][:].rearrange("p (h w) -> p h w", w=WW), wbd[conv][:, tap, :],
                                src[:, k * ROWS + dy:k * ROWS + dy + ROWS, dx:dx + WW],
                                start=tap == 0, stop=tap == 8)
                        mm.then_inc(summed, 1)

                @block.scalar
                def _(act):
                    for n in range(2 * CHUNKS):
                        conv = n // CHUNKS
                        act.wait_ge(summed, n + 1)
                        if n >= 2:
                            act.wait_ge(leaky, n - 1)
                        nc.scalar.activation(biased[:, n % 2, :], banks[n % 8][:], ACT.Identity,
                                             bias=bias[:, conv:conv + 1]).then_inc(plus_bias, 1)

                @block.vector
                def _(dve):
                    for n in range(2 * CHUNKS):
                        conv, k = n // CHUNKS, n % CHUNKS
                        dve.wait_ge(plus_bias, n + 1)
                        src = biased[:, n % 2, :]
                        if conv == 0:
                            dst = ypad[:, 1 + k * ROWS:1 + (k + 1) * ROWS, 1:1 + WW]
                            src = src.rearrange("p (h w) -> p h w", w=WW)
                        else:
                            dst = seq[:, k % 2, :]
                            if k >= 2:
                                dve.wait_ge(stored[k % 2], 16 * (k // 2))
                        nc.vector.scalar_tensor_tensor(out=dst, in0=src, scalar=LEAK, in1=src, op0=ALU.mult,
                                                       op1=ALU.max).then_inc(leaky, 1)
            clear(nc, [loaded, summed, plus_bias, leaky, *stored])

        with nc.Fori(0, PAIRS) as p:
            pair(p)


def pipeline(nc, banks, seq_d, scratch, w_in, cw, cb, w_dt_t, w_dt, dt_b, w_b, w_c, a_log, skip,
             w_out, w_cam_t, w_q4, w_k4, w_v, w_bn1_t, w_bn2_t, consts, out):
    x1_d, s1q_d, t2q_d, s1k_d, t2k_d, vt_d = scratch
    SA, SB, ACC, DEN, DPS, UPS, YPS, AUX = banks
    with ExitStack() as ctx:
        def sb(name, shape, dt=F32):
            return ctx.enter_context(nc.sbuf_tensor(name, shape, dt))

        def sem(name):
            return ctx.enter_context(nc.semaphore(name))

        cst = sb("cst", [P, C_END])
        selb = sb("selb", [P, GPB, P], BF16)
        win = sb("win", [P, 2 * D_INNER])
        wdt = sb("wdt", [P, D_INNER])
        wb = sb("wb", [P, P])
        wc = sb("wc", [P, P])
        wout = sb("wout", [P, CH])
        wq = sb("wq", [P, P])
        wk = sb("wk", [P, P])
        wxv = sb("wxv", [P, 2 * CH])
        wbn1 = sb("wbn1", [CH, CH])
        mixw = sb("mixw", [P, CH])
        small = sb("small", [P, 8 + 2 * GROUPS])
        taps, convb, dtb, dskip = small[:, 0:4], small[:, 4:5], small[:, 5:6], small[:, 6:7]
        alog, amat = small[:, 8:8 + GROUPS], small[:, 8 + GROUPS:8 + 2 * GROUPS]
        ones = sb("ones", [P, 32])
        ident = cst[:, C_ID:C_ID + P]
        seqt = sb("seqt", [P, 2, CHUNK])
        xin = sb("xin", [P, 2, CHUNK + D_CONV - 1])
        zraw = sb("zraw", [P, CHUNK])
        cacc = sb("cacc", [P, CHUNK])
        u = sb("u", [P, 2, CHUNK])
        zs = sb("zs", [P, 2, CHUNK])
        bbc = sb("bbc", [P, 2, CHUNK])
        cbc = sb("cbc", [P, 2, CHUNK])
        dtx = sb("dtx", [P, CHUNK])
        em = sb("em", [P, CHUNK])
        em1 = sb("em1", [P, CHUNK])
        lnm = sb("lnm", [P, CHUNK])
        low = sb("low", [P, CHUNK])
        dsp = sb("dsp", [P, 3, CHUNK])
        usp = sb("usp", [P, 3, CHUNK])
        stk = sb("stk", [96, 2, 2, BLOCKS, CHUNK])
        dA = sb("dA", [P, 2, CHUNK])
        hst = sb("hst", [P, SRING, CHUNK])
        carry = sb("carry", [P, GROUPS])
        hc = sb("hc", [P, HRING, CHUNK])
        ysb = sb("ysb", [P, CHUNK])
        y2 = sb("y2", [P, CHUNK])
        x1c = sb("x1c", [P, 2, CHUNK])
        full = sb("full", [P, 2, CHUNK])
        head = sb("head", [P, 2, CHUNK], BF16)
        rest = sb("rest", [CH, 2, CHUNK])
        mid = sb("mid", [CH, 2, CHUNK], BF16)
        s1st = sb("s1st", [P, 2, CHUNK], BF16)
        t2st = sb("t2st", [CH, 2, CHUNK], BF16)
        xv = sb("xv", [P, 4, 2 * CH])
        energy = sb("energy", [CH, CH])
        s1k = sb("s1k", [P, L], BF16)
        t2k = sb("t2k", [P, L], BF16)
        s1q = sb("s1q", [P, 3, QUARTER], BF16)
        t2q = sb("t2q", [P, 3, QUARTER], BF16)
        vt = sb("vt", [P, KT, CH])
        pr = sb("pr", [P, PRING, 2, CHUNK])
        x1a = sb("x1a", [P, 2, QUARTER])
        mxp = sb("mxp", [P, NT, CHUNKS])
        mx = sb("mx", [P, NT])
        nmx = sb("nmx", [NT, 3, P])
        nm3 = sb("nm3", [NT, 3, P], BF16)
        accs = sb("accs", [P, CHUNK])
        dens = sb("dens", [P, CHUNK])
        rinv = dens
        res = sb("res", [P, CHUNK])
        catt = sb("catt", [CH, CH])
        cst1 = sb("cst1", [CH, 4])

        zeroed, got, capped, made, wps, wdone = (
            sem(n) for n in ("zeroed", "got", "capped", "made", "wps", "wdone"))
        wdtt = dA[0:DT_RANK, 0, 0:P]
        wdt4 = dA[0:DT_RANK, 1, 0:P]
        wvt = dA[0:CH, 0, P:P + CH]
        wbn2 = dA[0:CH, 1, P:P + CH]
        loads = [(cst[:], consts), (win[0:CH, :], w_in), (wb[:], w_b), (wc[:], w_c), (wout[:], w_out),
                 (wq[0:CH, :], w_q4), (wk[0:CH, :], w_k4), (wxv[0:CH, 0:CH], w_cam_t), (wbn1[:], w_bn1_t),
                 (taps, cw), (convb, cb), (dtb, dt_b), (dskip, skip), (alog, a_log),
                 (wdtt, w_dt_t), (wdt4, w_dt), (wvt, w_v), (wbn2, w_bn2_t)]
        zero = [win, wq, wk, wxv, mixw, seqt, x1c, x1a]
        with nc.Block() as block:
            @block.vector
            def _(dve):
                for t in zero:
                    nc.vector.memset(t[CH:P], 0.0)
                nc.vector.memset(ones[:], 1.0).then_inc(zeroed, 1)
                dve.wait_ge(got, 16 * len(loads))
                nc.vector.tensor_scalar(alog, alog, A_LOG_MAX, None, ALU.min).then_inc(capped, 1)

            @block.gpsimd
            def _(pool):
                nc.gpsimd.memset(t2k[CH:P, :], 0.0).then_inc(made, 1)
                nc.gpsimd.memset(t2q[CH:P, :, :], 0.0)
                pool.wait_ge(made, 1)
                nc.gpsimd.memset(t2k[CH:CH + 3, :], 1.0)

            @block.sync
            def _(sp):
                for dst, src in loads:
                    sp.dma_start(dst, src).then_inc(got, 16)
                sp.wait_ge(got, 16 * len(loads))

            @block.tensor
            def _(pe):
                pe.wait_ge(got, 16 * len(loads))
                nc.tensor.matmul(AUX[:, 0:P], wdtt, wdt4, start=True, stop=True).then_inc(wps, 1)
                nc.tensor.matmul(YPS[0:CH, 0:CH], wvt, wbn2, start=True, stop=True).then_inc(wps, 1)

            @block.scalar
            def _(act):
                act.wait_ge(got, 16 * len(loads))
                act.wait_ge(capped, 1)
                nc.scalar.copy(selb[:].rearrange("p g n -> p (g n)"), cst[:, C_SEL:C_SUM])
                nc.scalar.activation(amat, alog, ACT.Exp).then_inc(wdone, 1)
                act.wait_ge(wdone, 1)
                nc.scalar.mul(amat, amat, -1.0)
                act.wait_ge(wps, 2)
                nc.scalar.copy(wdt[:], AUX[:, 0:P])
                nc.scalar.copy(wxv[0:CH, CH:2 * CH], YPS[0:CH, 0:CH])
        clear(nc, [zeroed, got, capped, made, wps, wdone])

        names = """seq0 seq1 xin_in conv silu em_in em1_in ln_in delta_in
                   du_in dres ures stk0 stk1 d_full da_in u_full dbu_in scan carried hc_in y_mm y_in y2_in
                   st_x1 qk_in rest_in mid_in split st_split st_vt aux_full aux_free
                   s_full p_full pv den ld_k ld_t ld_v ld_q0 ld_q1 ld_q2 ld_x0 ld_x1 max_in cexp nm3_in
                   nm_row acc_in st_out catt_in dstep astep gstep""".split()
        S = {n: sem(n) for n in names}

        def image(mamba, attn, i_m, i_a):
            first, last = -LEAD, TICKS + TAIL
            number, count = {}, 0
            for T in range(first, last):
                for e in events_of_tick(T, mamba, attn):
                    number[e] = count
                    count += 1

            def full_wait(eng, e):
                eng.wait_ge(S["aux_full"], number[e] + 1)

            def copied(eng, e):
                eng.wait_ge(S["aux_free"], number[e] + 1)

            with nc.Block() as block:
                @block.sync
                def _(sp):
                    def load_seq(c):
                        sp.dma_start(seqt[0:CH, c % 2, :], seq_d[bass.ds(i_m, 1)].rearrange("a c l -> (a c) l")
                                     [:, c * CHUNK:(c + 1) * CHUNK]).then_inc(S[f"seq{c % 2}"], 16)

                    def load_q(q):
                        cols = slice(q * QUARTER, (q + 1) * QUARTER)
                        sp.dma_start(s1q[:, q % 3, :], s1q_d[:, cols]).then_inc(S[f"ld_q{q % 3}"], 16)
                        sp.dma_start(t2q[0:CH, q % 3, :], t2q_d[:, cols]).then_inc(S[f"ld_q{q % 3}"], 16)

                    def load_x1(q):
                        sp.dma_start(x1a[0:CH, q % 2, :], x1_d[:, q * QUARTER:(q + 1) * QUARTER]).then_inc(
                            S[f"ld_x{q % 2}"], 16)

                    if mamba:
                        load_seq(0)
                        load_seq(1)
                    if attn:
                        load_q(0)
                        for k in range(QUARTERS):
                            cols = slice(k * QUARTER, (k + 1) * QUARTER)
                            sp.dma_start(s1k[:, cols], s1k_d[:, cols]).then_inc(S["ld_k"], 16)
                        sp.dma_start(t2k[0:CH, :], t2k_d).then_inc(S["ld_t"], 16)
                        sp.dma_start(vt[:], vt_d).then_inc(S["ld_v"], 16)
                        load_q(1)
                        load_x1(0)
                        load_x1(1)
                    for T in range(first, last):
                        if mamba:
                            c, r = T // GROUPS + 1, T % GROUPS
                            if c < CHUNKS and r == 3 and c + 2 < CHUNKS:
                                full_wait(sp, ("z", c))
                                load_seq(c + 2)
                            if c < CHUNKS and r in (12, 13):
                                w = r - 12
                                if r == 12:
                                    if c >= 2:
                                        sp.wait_ge(S["u_full"], GROUPS * (c - 1))
                                    sp.wait_ge(S["dres"], c + 1)
                                else:
                                    sp.wait_ge(S["ures"], c + 1)
                                src = (dsp, usp)[w]
                                for s in range(3):
                                    for j in range(BLOCKS):
                                        sp.dma_start(stk[BLOCK * s:BLOCK * (s + 1), c % 2, w, j, :],
                                                     src[BLOCK * j:BLOCK * (j + 1), s, :]).then_inc(
                                            S[f"stk{c % 2}"], 16)
                            c = T // GROUPS - 1
                            if c >= 0:
                                cols = slice(c * CHUNK, (c + 1) * CHUNK)
                                if r == 4:
                                    if attn and c == 0:
                                        sp.wait_ge(S["ld_x0"], 16)
                                    if attn:
                                        q = c // 2
                                        sp.wait_ge(S[f"ld_x{q % 2}"], 16 * (q // 2 + 1))
                                    copied(sp, ("out", c))
                                    sp.dma_start(x1_d[:, cols], x1c[0:CH, c % 2, :]).then_inc(S["st_x1"], 16)
                                if r == 9:
                                    if attn:
                                        q = c // 2
                                        sp.wait_ge(S[f"ld_q{q % 3}"], 32 * (q // 3 + 1))
                                        sp.wait_ge(S["ld_k"], 16 * QUARTERS)
                                        sp.wait_ge(S["ld_t"], 16)
                                    sp.wait_ge(S["split"], 4 * (c + 1))
                                    for w, (s1_d, t2_d) in enumerate(((s1q_d, t2q_d), (s1k_d, t2k_d))):
                                        sp.dma_start(s1_d[:, cols], s1st[:, w, :]).then_inc(S["st_split"], 16)
                                        sp.dma_start(t2_d[:, cols], t2st[:, w, :]).then_inc(S["st_split"], 16)
                                if r == 10:
                                    if attn:
                                        sp.wait_ge(S["ld_v"], 16)
                                    copied(sp, ("xv", c))
                                    sp.dma_start(vt_d[:, 4 * c:4 * (c + 1), :], xv[:, :, CH:2 * CH]).then_inc(
                                        S["st_vt"], 16)
                        if attn:
                            q, t = T // KT, T % KT
                            if T >= 0 and t == 2 and q + 2 < QUARTERS:
                                sp.wait_ge(S["s_full"], 2 * KT * q)
                                load_q(q + 2)
                            if T >= KT and t == 6:
                                full_wait(sp, ("res", q - 1))
                                if q + 1 < QUARTERS:
                                    load_x1(q + 1)
                                copied(sp, ("res", q - 1))
                                for h in range(2):
                                    a = (q - 1) * QUARTER + h * CHUNK
                                    sp.dma_start(out[bass.ds(i_a, 1)].rearrange("a c l -> (a c) l")
                                                 [:, a:a + CHUNK], res[CH * h:CH * (h + 1), :]).then_inc(
                                        S["st_out"], 16)
                            q, t = (0, T + LEAD - (LEAD - 4)) if T < 0 else (q + 1, t - MAX_TICKS)
                            if q < QUARTERS and t == 2:
                                sp.wait_ge(S["nm3_in"], q + 1)
                                sp.wait_ge(S[f"ld_q{q % 3}"], 32 * (q // 3 + 1))
                                for s in range(3):
                                    sp.dma_start(t2q[CH + s:CH + s + 1, q % 3, :], nm3[:, s, :]).then_inc(
                                        S["nm_row"], 16)
                    if mamba:
                        sp.wait_ge(S["st_x1"], 16 * CHUNKS)
                        sp.wait_ge(S["st_split"], 64 * CHUNKS)
                        sp.wait_ge(S["st_vt"], 16 * CHUNKS)
                    if attn:
                        sp.wait_ge(S["st_out"], 32 * QUARTERS)

                @block.tensor
                def _(pe):
                    def event(e):
                        n = number[e]
                        if n:
                            pe.wait_ge(S["aux_free"], n)
                        kind, c = e[0], e[-1]
                        A = AUX
                        if kind == "max":
                            q, k = e[1], e[2]
                            nt, mc = k // CHUNKS, k % CHUNKS
                            if k == 0:
                                pe.wait_ge(S[f"ld_q{q % 3}"], 32 * (q // 3 + 1))
                            if q == 0 and nt == 0 and mc % 2 == 0:
                                pe.wait_ge(S["ld_k"], 16 * QUARTERS)
                            mm = nc.tensor.matmul(A[:], s1q[:, q % 3, nt * P:(nt + 1) * P],
                                                  s1k[:, mc * CHUNK:(mc + 1) * CHUNK], start=True, stop=True)
                        elif kind == "turn":
                            pe.wait_ge(S["max_in"], c + 1)
                            mm = nc.tensor.matmul(A[0:NT, 0:P], mx[:], ident, start=True, stop=True)
                        elif kind == "mix":
                            pe.wait_ge(S["catt_in"], 1)
                            mm = nc.tensor.matmul(A[0:CH, 0:CH], catt[:], wbn1[:], start=True, stop=True)
                        elif kind == "den":
                            pe.wait_ge(S["acc_in"], 2 * (c + 1))
                            mm = nc.tensor.matmul(A[:], cst[:, C_DEN:C_DEN + P], dens[:], start=True, stop=True)
                        elif kind == "res":
                            pe.wait_ge(S[f"ld_x{c % 2}"], 16 * (c // 2 + 1))
                            copied(pe, ("mix",))
                            for h in range(2):
                                mm = nc.tensor.matmul(A[CH * h:CH * (h + 1), :], mixw[:],
                                                      x1a[:, c % 2, h * CHUNK:(h + 1) * CHUNK],
                                                      start=True, stop=True)
                        elif kind in ("xin", "z"):
                            if kind == "xin":
                                pe.wait_ge(S[f"seq{c % 2}"], 16 * (c // 2 + 1))
                            o = 0 if kind == "xin" else D_INNER
                            mm = nc.tensor.matmul(A[:], win[:, o:o + D_INNER], seqt[:, c % 2, :],
                                                  start=True, stop=True)
                        elif kind in ("dt", "B", "C"):
                            pe.wait_ge(S["silu"], 2 * (c + 1))
                            w = {"dt": wdt, "B": wb, "C": wc}[kind]
                            mm = nc.tensor.matmul(A[:], w[:], u[:, c % 2, :], start=True, stop=True)
                        elif kind == "out":
                            pe.wait_ge(S["y2_in"], c + 1)
                            mm = nc.tensor.matmul(A[0:CH, :], wout[:], y2[:], start=True, stop=True)
                        elif kind in ("q", "k"):
                            copied(pe, ("out", c))
                            mm = nc.tensor.matmul(A[:], (wq if kind == "q" else wk)[:], x1c[:, c % 2, :],
                                                  start=True, stop=True)
                        elif kind == "xv":
                            for t in range(4):
                                mm = nc.tensor.matmul(A[:, t * P:(t + 1) * P], x1c[:, c % 2, t * P:(t + 1) * P],
                                                      wxv[:], start=True, stop=True)
                        elif kind == "en":
                            copied(pe, ("xv", c))
                            for t in range(4):
                                mm = nc.tensor.matmul(A[0:CH, 0:CH], xv[:, t, 0:CH], xv[:, t, 0:CH],
                                                      start=t == 0, stop=t == 3)
                        mm.then_inc(S["aux_full"], 1)

                    def scores(T):
                        q, t = T // KT, T % KT
                        if t == 0:
                            pe.wait_ge(S["nm_row"], 48 * (q + 1))
                        if T == 0:
                            pe.wait_ge(S["ld_t"], 16)
                        for h, bank in enumerate((SA, SB)):
                            if T >= 1:
                                pe.wait_ge(S["p_full"], 2 * T - 1 + h)
                            cols = slice(h * CHUNK, (h + 1) * CHUNK)
                            nc.tensor.matmul(bank[:], s1k[:, t * P:(t + 1) * P], s1q[:, q % 3, cols],
                                             start=True, stop=False)
                            nc.tensor.matmul(bank[:], t2k[:, t * P:(t + 1) * P], t2q[:, q % 3, cols],
                                             start=False, stop=True).then_inc(S["s_full"], 1)

                    def values(T):
                        q, t = T // KT, T % KT
                        pe.wait_ge(S["p_full"], 2 * T + 2)
                        if T == 0:
                            pe.wait_ge(S["ld_v"], 16)
                        if t == 0 and q:
                            pe.wait_ge(S["acc_in"], 2 * q)
                        for h in range(2):
                            mm = nc.tensor.matmul(ACC[CH * h:CH * (h + 1), :], vt[:, t, :],
                                                  pr[:, T % PRING, h, :], start=t == 0, stop=t == KT - 1)
                        mm.then_inc(S["pv"], 1)

                    def sums(T):
                        t = T % KT
                        for par in range(2):
                            for h in range(2):
                                o = 64 * par + 32 * h
                                mm = nc.tensor.matmul(DEN[o:o + 32, :], ones[:], pr[:, (T - 1 + par) % PRING, h, :],
                                                      start=t == 1, stop=t == KT - 1, tile_position=(0, o))
                        mm.then_inc(S["den"], 1)

                    def reduce_states(T):
                        g = T % GROUPS
                        if g == 0 and T:
                            pe.wait_ge(S["y_in"], T // GROUPS)
                        pe.wait_ge(S["hc_in"], T + 1)
                        j, gl = g // GPB, g % GPB
                        nc.tensor.matmul(YPS[BLOCK * j:BLOCK * (j + 1), :],
                                         cst[:, C_SUM + BLOCK * gl:C_SUM + BLOCK * (gl + 1)], hc[:, T % HRING, :],
                                         start=gl == 0, stop=gl == GPB - 1,
                                         tile_position=(0, BLOCK * j)).then_inc(S["y_mm"], 1)

                    def spread(T):
                        c, g = T // GROUPS, T % GROUPS
                        j, gl = g // GPB, g % GPB
                        if g == 0:
                            pe.wait_ge(S[f"stk{c % 2}"], 16 * 6 * BLOCKS * (c // 2 + 1))
                        if T:
                            pe.wait_ge(S["da_in"], T)
                        nc.tensor.matmul(DPS[:], selb[0:96, gl, :],
                                         stk[:, c % 2, 0, j, :].bitcast(BF16)[:, 1::2],
                                         start=True, stop=True).then_inc(S["d_full"], 1)
                        if T:
                            pe.wait_ge(S["scan"], T)
                        nc.tensor.matmul(UPS[:], selb[0:96, gl, :],
                                         stk[:, c % 2, 1, j, :].bitcast(BF16)[:, 1::2],
                                         start=True, stop=True).then_inc(S["u_full"], 1)

                    for T in range(first, last):
                        ev = events_of_tick(T, mamba, attn)
                        if attn and 0 <= T < TICKS:
                            scores(T)
                        for e in ev[0:1]:
                            event(e)
                        if attn and 1 <= T <= TICKS:
                            values(T - 1)
                        for e in ev[1:2]:
                            event(e)
                        if attn and 1 <= T <= TICKS and T % 2 == 0:
                            sums(T - 1)
                        if mamba and 2 <= T < TICKS + 2:
                            reduce_states(T - 2)
                        for e in ev[2:3]:
                            event(e)
                        if mamba and 0 <= T + 1 < TICKS:
                            spread(T + 1)
                        for e in ev[3:]:
                            event(e)

                @block.scalar
                def _(act):
                    def link(ins, n=[0]):
                        n[0] += 1
                        ins.then_inc(S["astep"], 1)
                        act.wait_ge(S["astep"], n[0])

                    def event(e):
                        kind, c = e[0], e[-1]
                        if kind == "xin":
                            if c:
                                if c >= 2:
                                    act.wait_ge(S["conv"], c - 1)
                                nc.scalar.copy(xin[:, c % 2, 0:D_CONV - 1],
                                               xin[:, (c - 1) % 2, CHUNK:CHUNK + D_CONV - 1]).then_inc(
                                    S["xin_in"], 1)
                            full_wait(act, e)
                            nc.scalar.copy(xin[:, c % 2, D_CONV - 1:], AUX[:]).then_inc(S["aux_free"], 1)
                            copied(act, e)
                        elif kind == "z":
                            full_wait(act, e)
                            nc.scalar.copy(zraw[:], AUX[:]).then_inc(S["aux_free"], 1)
                            copied(act, e)
                        elif kind == "dt":
                            if c:
                                act.wait_ge(S["delta_in"], c)
                            full_wait(act, e)
                            nc.scalar.activation(dtx[:], AUX[:], ACT.Identity, bias=dtb).then_inc(S["aux_free"], 1)
                            copied(act, e)
                        elif kind in ("B", "C"):
                            if c >= 2:
                                act.wait_ge(S["dbu_in" if kind == "B" else "hc_in"], GROUPS * (c - 1))
                            full_wait(act, e)
                            nc.scalar.copy((bbc if kind == "B" else cbc)[:, c % 2, :], AUX[:]).then_inc(
                                S["aux_free"], 1)
                        elif kind == "out":
                            if c:
                                act.wait_ge(S["st_x1"], 16 * c)
                            full_wait(act, e)
                            nc.scalar.copy(x1c[0:CH, c % 2, :], AUX[0:CH, :]).then_inc(S["aux_free"], 1)
                        elif kind in ("q", "k"):
                            w = 0 if kind == "q" else 1
                            if c:
                                act.wait_ge(S["split"], 4 * c)
                            full_wait(act, e)
                            nc.scalar.copy(full[:, w, :], AUX[:]).then_inc(S["aux_free"], 1)
                            copied(act, e)
                            nc.scalar.copy(head[:, w, :], full[:, w, :]).then_inc(S["qk_in"], 1)
                        elif kind == "xv":
                            if c:
                                copied(act, ("en", c - 1))
                                act.wait_ge(S["st_vt"], 16 * c)
                            full_wait(act, e)
                            nc.scalar.copy(xv[:].rearrange("p t n -> p (t n)"), AUX[:]).then_inc(S["aux_free"], 1)

                    for T in range(first, last):
                        if attn and T == first:
                            act.wait_ge(S["dstep"], 1)
                            nc.scalar.activation(catt[:], energy[:], ACT.Exp, bias=cst1[:, 0:1],
                                                 accum_out=cst1[:, 1:2]).then_inc(S["cexp"], 1)
                        if attn and 0 <= T < TICKS:
                            if T >= PRING:
                                act.wait_ge(S["pv"], T - PRING + 1)
                                act.wait_ge(S["den"], (T - PRING) // 2 + 1)
                            for h, bank in enumerate((SA, SB)):
                                act.wait_ge(S["s_full"], 2 * T + h + 1)
                                nc.scalar.activation(pr[:, T % PRING, h, :], bank[:], ACT.Exp).then_inc(
                                    S["p_full"], 1)
                        if mamba and 0 <= T < TICKS:
                            act.wait_ge(S["d_full"], T + 1)
                            if T >= 2:
                                act.wait_ge(S["scan"], T - 1)
                            nc.scalar.activation(dA[:, T % 2, :], DPS[:], ACT.Exp,
                                                 scale=amat[:, T % GROUPS:T % GROUPS + 1]).then_inc(S["da_in"], 1)
                        if mamba and 1 <= T <= TICKS:
                            act.wait_ge(S["scan"], T)
                            nc.scalar.copy(carry[:, (T - 1) % GROUPS:(T - 1) % GROUPS + 1],
                                           hst[:, (T - 1) % SRING, CHUNK - 1:CHUNK]).then_inc(S["carried"], 1)
                        for e in events_of_tick(T, mamba, attn):
                            event(e)
                        if mamba:
                            c, r = T // GROUPS + 1, T % GROUPS
                            if c < CHUNKS and r == 5:
                                if c >= 2:
                                    act.wait_ge(S["y2_in"], c - 1)
                                nc.scalar.activation(zs[:, c % 2, :], zraw[:], ACT.Silu).then_inc(S["silu"], 1)
                                act.wait_ge(S["conv"], c + 1)
                                nc.scalar.activation(u[:, c % 2, :], cacc[:], ACT.Silu).then_inc(S["silu"], 1)
                            if c < CHUNKS and r == 8:
                                link(nc.scalar.activation(em[:], dtx[:], ACT.Abs))
                                nc.scalar.activation(em[:], em[:], ACT.Exp, scale=-1.0).then_inc(S["em_in"], 1)
                                act.wait_ge(S["em1_in"], c + 1)
                                nc.scalar.activation(lnm[:], em1[:], ACT.Ln).then_inc(S["ln_in"], 1)
                            c = T // GROUPS - 1
                            if c >= 0 and r == 7:
                                for w in range(2):
                                    act.wait_ge(S["rest_in"], 2 * c + w + 1)
                                    nc.scalar.copy(mid[:, w, :], rest[:, w, :]).then_inc(S["mid_in"], 1)

                @block.vector
                def _(dve):
                    steps = [0]

                    def link(ins):
                        steps[0] += 1
                        ins.then_inc(S["dstep"], 1)
                        dve.wait_ge(S["dstep"], steps[0])

                    def event(e):
                        kind, c = e[0], e[-1]
                        if kind == "max":
                            q, k = e[1], e[2]
                            full_wait(dve, e)
                            nc.vector.reduce_max(mxp[:, k // CHUNKS, k % CHUNKS:k % CHUNKS + 1], AUX[:],
                                                 AX_X).then_inc(S["aux_free"], 1)
                            if k == NT * CHUNKS - 1:
                                copied(dve, e)
                                nc.vector.tensor_reduce(mx[:], mxp[:], AX_X, ALU.max).then_inc(S["max_in"], 1)
                        elif kind == "turn":
                            full_wait(dve, e)
                            if c:
                                dve.wait_ge(S["nm_row"], 48 * c)
                            nc.vector.tensor_scalar(nmx[:, 0, :], AUX[0:NT, 0:P], -1.0, None,
                                                    ALU.mult).then_inc(S["aux_free"], 1)
                            copied(dve, e)
                            link(nc.vector.tensor_copy(nm3[:, 0, :], nmx[:, 0, :]))
                            link(nc.vector.tensor_tensor(nmx[:, 1, :], nmx[:, 0, :], nm3[:, 0, :], ALU.subtract))
                            link(nc.vector.tensor_copy(nm3[:, 1, :], nmx[:, 1, :]))
                            nc.vector.tensor_tensor(nm3[:, 2, :], nmx[:, 1, :], nm3[:, 1, :],
                                                    ALU.subtract).then_inc(S["nm3_in"], 1)
                        elif kind == "mix":
                            full_wait(dve, e)
                            nc.vector.tensor_tensor(mixw[0:CH, :], AUX[0:CH, 0:CH], cst[0:CH, C_ID:C_ID + CH],
                                                    ALU.add).then_inc(S["aux_free"], 1)
                        elif kind == "den":
                            full_wait(dve, e)
                            nc.vector.reciprocal(rinv[:], AUX[:]).then_inc(S["aux_free"], 1)
                            copied(dve, e)
                            link(nc.vector.tensor_tensor(accs[:], accs[:], rinv[:], ALU.mult))
                        elif kind == "res":
                            full_wait(dve, e)
                            if c:
                                dve.wait_ge(S["st_out"], 32 * c)
                            nc.vector.tensor_tensor(res[:], accs[:], AUX[:], ALU.add).then_inc(S["aux_free"], 1)
                        elif kind == "en":
                            full_wait(dve, e)
                            if c == 0:
                                ins = nc.vector.tensor_copy(energy[:], AUX[0:CH, 0:CH])
                            else:
                                copied(dve, ("en", c - 1))
                                ins = nc.vector.tensor_tensor(energy[:], energy[:], AUX[0:CH, 0:CH], ALU.add)
                            ins.then_inc(S["aux_free"], 1)

                    def hi(t):
                        return t.bitcast(BF16)[:, 1::2]

                    for T in range(first, last):
                        if attn and T == first:
                            link(nc.vector.tensor_reduce(cst1[:, 0:1], energy[:], AX_X, ALU.max, negate=True))
                            dve.wait_ge(S["cexp"], 1)
                            link(nc.vector.reciprocal(cst1[:, 2:3], cst1[:, 1:2]))
                            nc.vector.tensor_scalar(catt[:], catt[:], cst1[:, 2:3], None, ALU.mult).then_inc(
                                S["catt_in"], 1)
                        ev = events_of_tick(T, mamba, attn)
                        c0, r = T // GROUPS, T % GROUPS
                        if attn and T >= KT and T % KT == 1:
                            q = T // KT
                            dve.wait_ge(S["pv"], KT * q)
                            if q >= 2:
                                copied(dve, ("res", q - 2))
                            nc.vector.tensor_copy(accs[:], ACC[:]).then_inc(S["acc_in"], 1)
                            dve.wait_ge(S["den"], KT * q // 2)
                            nc.vector.tensor_copy(dens[:], DEN[:]).then_inc(S["acc_in"], 1)
                        if mamba and c0 - 1 >= 0 and r == 2:
                            c = c0 - 1
                            dve.wait_ge(S["y_mm"], GROUPS * (c + 1))
                            if c:
                                dve.wait_ge(S["y2_in"], c)
                            nc.vector.scalar_tensor_tensor(out=ysb[:], in0=u[:, c % 2, :], scalar=dskip, in1=YPS[:],
                                                           op0=ALU.mult, op1=ALU.add).then_inc(S["y_in"], 1)
                        if mamba and 0 <= T < TICKS:
                            dve.wait_ge(S["u_full"], T + 1)
                            if r == 0:
                                copied(dve, ("B", c0))
                            nc.vector.tensor_tensor(UPS[:], UPS[:], bbc[:, c0 % 2, :], ALU.mult).then_inc(
                                S["dbu_in"], 1)
                        for e in ev[0:1]:
                            event(e)
                        if mamba and 0 <= T < TICKS:
                            g = T % GROUPS
                            dve.wait_ge(S["dbu_in"], T + 1)
                            dve.wait_ge(S["da_in"], T + 1)
                            if T >= SRING:
                                dve.wait_ge(S["hc_in"], T - SRING + 1)
                                dve.wait_ge(S["carried"], T - SRING + 1)
                            nc.vector.tensor_tensor_scan(
                                hst[:, T % SRING, :], dA[:, T % 2, :], UPS[:],
                                carry[:, g:g + 1] if c0 else 0.0, ALU.mult, ALU.add).then_inc(
                                S["scan"], 1)
                        for e in ev[1:]:
                            event(e)
                        if mamba:
                            c = c0 + 1
                            if c < CHUNKS and r == 0 and c == 0:
                                nc.vector.memset(xin[:, 0, 0:D_CONV - 1], 0.0).then_inc(S["xin_in"], 1)
                            if c < CHUNKS and r in (3, 4):
                                x_ = xin[:, c % 2, :]
                                if r == 3:
                                    dve.wait_ge(S["xin_in"], c + 1)
                                    copied(dve, ("xin", c))
                                    if c:
                                        dve.wait_ge(S["silu"], 2 * c)
                                    link(nc.vector.tensor_scalar(cacc[:], x_[:, 0:CHUNK], taps[:, 0:1], convb,
                                                                 ALU.mult, ALU.add))
                                for k in ((1,), (2, 3))[r - 3]:
                                    ins = nc.vector.scalar_tensor_tensor(
                                        out=cacc[:], in0=x_[:, k:k + CHUNK], scalar=taps[:, k:k + 1], in1=cacc[:],
                                        op0=ALU.mult, op1=ALU.add)
                                    if k < D_CONV - 1:
                                        link(ins)
                                    else:
                                        ins.then_inc(S["conv"], 1)
                            if c < CHUNKS and r == 8:
                                dve.wait_ge(S["em_in"], c + 1)
                                nc.vector.tensor_scalar(em1[:], em[:], 1.0, None, ALU.add).then_inc(S["em1_in"], 1)
                                dve.wait_ge(S["em1_in"], c + 1)
                                link(nc.vector.scalar_tensor_tensor(out=low[:], in0=em1[:], scalar=1.0, in1=em[:],
                                                                    op0=ALU.subtract, op1=ALU.subtract))
                            if c < CHUNKS and r == 9:
                                dve.wait_ge(S["ln_in"], c + 1)
                                link(nc.vector.tensor_tensor(low[:], lnm[:], low[:], ALU.subtract))
                                if c:
                                    dve.wait_ge(S[f"stk{(c - 1) % 2}"], 16 * 6 * BLOCKS * ((c - 1) // 2 + 1))
                                nc.vector.scalar_tensor_tensor(out=dsp[:, 0, :], in0=dtx[:], scalar=0.0, in1=low[:],
                                                               op0=ALU.max, op1=ALU.add).then_inc(S["delta_in"], 1)
                                dve.wait_ge(S["delta_in"], c + 1)
                                nc.vector.tensor_tensor(usp[:, 0, :], dsp[:, 0, :], u[:, c % 2, :],
                                                        ALU.mult).then_inc(S["du_in"], 1)
                            if c < CHUNKS and r == 10:
                                link(nc.vector.tensor_tensor(dsp[:, 1, :], dsp[:, 0, :], hi(dsp[:, 0, :]),
                                                             ALU.subtract))
                                nc.vector.tensor_tensor(dsp[:, 2, :], dsp[:, 1, :], hi(dsp[:, 1, :]),
                                                        ALU.subtract).then_inc(S["dres"], 1)
                            c = c0 - 1
                            if c >= 0 and r in (6, 7, 8):
                                for w in range(2):
                                    m1 = cst[:, C_MASK + w:C_MASK + w + 1]
                                    m2 = cst[0:CH, C_MASK + 2 + w:C_MASK + 3 + w]
                                    if r == 6:
                                        dve.wait_ge(S["qk_in"], 2 * c + w + 1)
                                        if c:
                                            dve.wait_ge(S["st_split"], 64 * c)
                                        nc.vector.scalar_tensor_tensor(
                                            out=rest[:, w, :], in0=head[0:CH, w, :], scalar=m2, in1=full[0:CH, w, :],
                                            op0=ALU.mult, op1=ALU.add).then_inc(S["rest_in"], 1)
                                    if r == 7:
                                        nc.vector.scalar_tensor_tensor(
                                            out=s1st[:, w, :], in0=head[:, w, :], scalar=m1, in1=full[:, w, :],
                                            op0=ALU.mult, op1=ALU.add).then_inc(S["split"], 1)
                                    if r == 8:
                                        dve.wait_ge(S["mid_in"], 2 * c + w + 1)
                                        nc.vector.scalar_tensor_tensor(
                                            out=t2st[:, w, :], in0=mid[:, w, :], scalar=m2, in1=rest[:, w, :],
                                            op0=ALU.mult, op1=ALU.add).then_inc(S["split"], 1)

                @block.gpsimd
                def _(pool):
                    if not mamba:
                        return

                    def hi(t):
                        return t.bitcast(BF16)[:, 1::2]

                    for T in range(first, last):
                        c0, r = T // GROUPS, T % GROUPS
                        if 0 <= T < TICKS:
                            if r == 0:
                                copied(pool, ("C", c0))
                            pool.wait_ge(S["scan"], T + 1)
                            if T >= HRING:
                                pool.wait_ge(S["y_mm"], T - HRING + 1)
                            nc.gpsimd.tensor_tensor(hc[:, T % HRING, :], hst[:, T % SRING, :], cbc[:, c0 % 2, :],
                                                    ALU.mult).then_inc(S["hc_in"], 1)
                        c = c0 - 1
                        if c >= 0 and r == 2:
                            pool.wait_ge(S["y_in"], c + 1)
                            if c:
                                full_wait(pool, ("out", c - 1))
                            nc.gpsimd.tensor_tensor(y2[:], ysb[:], zs[:, c % 2, :], ALU.mult).then_inc(
                                S["y2_in"], 1)
                        c = c0 + 1
                        if c < CHUNKS and r == 10:
                            pool.wait_ge(S["du_in"], c + 1)
                            nc.gpsimd.tensor_tensor(usp[:, 1, :], usp[:, 0, :], hi(usp[:, 0, :]),
                                                    ALU.subtract).then_inc(S["gstep"], 1)
                            pool.wait_ge(S["gstep"], c + 1)
                            nc.gpsimd.tensor_tensor(usp[:, 2, :], usp[:, 1, :], hi(usp[:, 1, :]),
                                                    ALU.subtract).then_inc(S["ures"], 1)
            clear(nc, list(S.values()))

        image(True, False, 0, None)
        with nc.Fori(1, IMAGES) as i:
            image(True, True, i, i - 1)
        image(False, True, None, IMAGES - 1)


def kernel(x, L0_conv_conv_w1, L0_conv_conv_b1, L0_conv_conv_w2, L0_conv_conv_b2, L0_conv_in_proj_w,
           L0_conv_conv1d_w, L0_conv_conv1d_b, L0_conv_x_proj_w, L0_conv_dt_proj_w, L0_conv_dt_proj_b,
           L0_conv_A_log, L0_conv_D, L0_conv_out_proj_w, L1_conv_w_cam, L1_conv_w_q, L1_conv_w_k,
           L1_conv_w_v, L1_conv_w_bn):
    import numpy as np
    import concourse.bacc as bacc
    from concourse.bass_utils import run_bass_kernel_spmd

    def taps_first(w):
        return np.asarray(w).reshape(CH, CH, 9).transpose(1, 2, 0)

    def lanes(w):
        return np.repeat(np.asarray(w), DL, axis=1)

    col = lambda v: np.asarray(v).reshape(-1, 1)
    xp = np.asarray(L0_conv_x_proj_w)
    bn = np.asarray(L1_conv_w_bn)
    arrays = dict(
        x=np.asarray(x).reshape(PAIRS, P, HH, WW),
        w1=taps_first(L0_conv_conv_w1), b1=col(L0_conv_conv_b1),
        w2=taps_first(L0_conv_conv_w2), b2=col(L0_conv_conv_b2),
        w_in=np.asarray(L0_conv_in_proj_w),
        cw=np.asarray(L0_conv_conv1d_w).reshape(D_INNER, D_CONV), cb=col(L0_conv_conv1d_b),
        w_dt_t=xp[:, 0:DT_RANK].T, w_dt=np.asarray(L0_conv_dt_proj_w), dt_b=col(L0_conv_dt_proj_b),
        w_b=lanes(xp[:, DT_RANK:DT_RANK + D_STATE]), w_c=lanes(xp[:, DT_RANK + D_STATE:]),
        a_log=np.asarray(L0_conv_A_log).reshape(GROUPS, DL, D_STATE).transpose(2, 1, 0).reshape(P, GROUPS),
        skip=col(L0_conv_D), w_out=np.asarray(L0_conv_out_proj_w),
        w_cam_t=np.asarray(L1_conv_w_cam).T,
        w_q4=np.tile(np.asarray(L1_conv_w_q).T, (1, 4)), w_k4=np.tile(np.asarray(L1_conv_w_k).T, (1, 4)),
        w_v=np.asarray(L1_conv_w_v), w_bn1_t=bn[:, 0:CH].T, w_bn2_t=bn[:, CH:].T,
        consts=shape_constants())
    nc = bacc.Bacc("TRN2", target_bir_lowering=False, num_devices=1)
    given, args = {}, {}
    for name, a in arrays.items():
        a = np.ascontiguousarray(a)
        given[f"in_{name}"] = a
        args[name] = nc.dram_tensor(f"in_{name}", a.shape, mybir.dt.from_np(a.dtype), kind="ExternalInput").ap()
    out = nc.dram_tensor("out_0", (IMAGES, CH, L), F32, kind="ExternalOutput").ap()
    build(nc, out=out, **args)
    r = run_bass_kernel_spmd(nc, [given], core_ids=[0])
    return r.results[0]["out_0"].reshape(IMAGES, CH, HH, WW)
```

```python
from contextlib import ExitStack

import concourse.bass as bass
from concourse import mybir

F32 = mybir.dt.float32
BF16 = mybir.dt.bfloat16
ALU = mybir.AluOpType
ACT = mybir.ActivationFunctionType
AX_X = mybir.AxisListType.X

P = 128
IMAGES, CH, HH, WW = 16, 64, 64, 64
L = HH * WW
PAIRS = IMAGES // 2
PAD = HH + 2
D_INNER, D_STATE, D_CONV, DT_RANK = 128, 16, 4, 4
LEAK = 0.01
A_LOG_MAX = 84.0
CHUNK = 512
CHUNKS = L // CHUNK
ROWS = CHUNK // WW
DL = P // D_STATE
GROUPS = D_INNER // DL
BLOCK = 32
BLOCKS = D_INNER // BLOCK
GPB = BLOCK // DL
QDIM = CH // 2
QUARTER = 1024
QUARTERS = L // QUARTER
KT = L // P
NT = QUARTER // P
TICKS = CHUNKS * GROUPS
assert TICKS == QUARTERS * KT
MAIN = 48
SEARCH = 18
QUARTER_LOAD = 16
KX_LOAD = 13
SPAN = 26
END = 8
PRING = 4
SRING = 4
HRING = 8

C_ID = 0
C_SEL = C_ID + P
C_SUM = C_SEL + GPB * P
C_DEN = C_SUM + GPB * BLOCK
C_MASK = C_DEN + P
C_END = C_MASK + 4


TRIED = [0]
for t in range(SPAN):
    TRIED.append(min(NT * CHUNKS, TRIED[t] + (3 if (SEARCH + t) % GROUPS in (0, 3, 4, 5, 8, 10, 13, 15) else 2)))
assert TRIED[SPAN] == NT * CHUNKS


def shape_constants():
    import numpy as np
    c = np.zeros((P, C_END), np.float32)
    c[:, C_ID:C_ID + P] = np.eye(P)
    for lane in range(P):
        for g in range(GPB):
            row = DL * g + lane % DL
            for s in range(3):
                c[BLOCK * s + row, C_SEL + P * g + lane] = 1
            c[lane, C_SUM + BLOCK * g + row] = 1
    for col in range(P):
        half = col // CH
        c[32 * half, C_DEN + col] = 1
        c[64 + 32 * half, C_DEN + col] = 1
    block = np.arange(P) // 32
    c[:, C_MASK] = -1.0 * (block >= 2)
    c[:, C_MASK + 1] = -1.0 * (block % 2 == 1)
    c[:, C_MASK + 2] = -1.0 * (block == 1)
    c[:, C_MASK + 3] = -1.0 * (block == 0)
    return c


def group_of(T):
    k = T % GROUPS
    return k % BLOCKS * GPB + k // BLOCKS


class Step:

    def __init__(self, j):
        self.now, self.next = 0 <= j < IMAGES, 0 <= j + 1 < IMAGES
        self.back = {d: 0 <= j - d < IMAGES for d in (1, 2)}
        self.first = -GROUPS if j == 0 else 0
        self.last = TICKS if j <= IMAGES else MAIN + END + 1
        self.uses, self.number, self.freed = [], {}, {}
        self.counts = {}
        for T in range(self.first, self.last):
            for e in self.plan(T):
                if e[0] in SIGNAL_OF:
                    self.note(SIGNAL_OF[e[0]], e[1:])
                    continue
                self.number[e] = len(self.uses)
                self.uses.append(e)
                signal = {"S": "p_full", "D": "da_in"}.get(e[0], "dve_took" if e[0] in DVE_USES else "act_took")
                self.freed[e] = (signal, self.note(signal, e))

    def note(self, name, event):
        c = self.counts.setdefault(name, {})
        c[event] = len(c) + 1
        return len(c)

    def prepares(self, c):
        return c < CHUNKS and self.now or c == CHUNKS and self.next

    def follows(self, c):
        return self.now if c >= 0 else self.back[1]

    def scans(self, T):
        return self.now and 0 <= T < TICKS

    def carries(self, T):
        return self.scans(T) and T < TICKS - GROUPS

    def spreads(self, T):
        return T >= 0 and T > self.first and self.prepares(T // GROUPS)

    def attends(self, T):
        d, lin = (1, T - MAIN) if T >= MAIN else (2, T - MAIN + TICKS)
        return (d, lin // KT, lin % KT) if self.back[d] and lin >= 0 and T < TICKS else None

    def ended(self, T):
        d, lin = (1, T - MAIN) if T > MAIN else (2, T - MAIN + TICKS)
        return (d, lin // KT - 1) if self.back[d] and lin % KT == 0 and lin >= KT else None

    @staticmethod
    def before(quarter):
        d, q = quarter
        return (d, q - 1) if q else (d + 1, QUARTERS - 1)

    def searches(self, T):
        d, lin = (1, T - SEARCH) if T >= SEARCH else (2, T - SEARCH + TICKS)
        return (d, lin // KT, lin % KT) if self.back[d] and lin >= 0 and T >= 0 else None

    def small_uses(self, T):
        ev = []
        found = self.searches(T)
        if found:
            d, q, t = found
            if t < SPAN:
                ev += [("max", (d, q), k) for k in range(TRIED[t], TRIED[t + 1])]
            if t == SPAN + 1:
                ev.append(("turn", (d, q)))
        if T == MAIN + 10 and self.back[1]:
            ev.append(("mix", 1))
        for lag, name in ((2, "den"), (7, "res")):
            done = self.ended(T - lag)
            if done and T - lag >= 0:
                ev.append((name, done))
        sl, r = T // GROUPS, T % GROUPS
        name = {0: "xin", 3: "z", 6: "dt", 7: "B", 11: "C"}.get(r)
        if name and self.prepares(sl + 1):
            ev.append((name, sl + 1))
        name = {5: "out", 9: "q", 10: "k", 12: "xv", 14: "en"}.get(r)
        if name and sl >= 0 and self.follows(sl - 1):
            ev.append((name, sl - 1))
        return ev

    def plan(self, T):
        uses, plan = self.small_uses(T), []
        if self.attends(T):
            plan += [("S", T, 0), ("S", T, 1)]
        if self.spreads(T + 1):
            plan.append(("D", T + 1))
        if T >= 0 and self.had(T - 1):
            plan.append(("PV", T - 1))
        if self.spreads(T + 1):
            plan.append(("U", T + 1))
        plan += uses[0:1]
        if T >= 0 and T % 2 == 0 and self.had(T - 1):
            plan.append(("SUM", T - 1))
        b = (T - BLOCKS - 1) // BLOCKS
        if (T - BLOCKS - 1) % BLOCKS == 0 and T >= 0 and (self.back[1] if b < 0 else self.now):
            plan.append(("Y", b))
        return plan + uses[1:]

    def had(self, T):
        return self.attends(T) if T >= 0 else (2, (TICKS - MAIN - 1) // KT, (TICKS - MAIN - 1) % KT) \
            if self.back[2] else None


SIGNAL_OF = {"PV": "pv", "U": "u_full", "SUM": "den", "Y": "y_mm"}
DVE_USES = ("max", "turn", "mix", "res", "en")
RING = 4


def build(nc, x, w1, b1, w2, b2, w_in, cw, cb, w_dt_t, w_dt, dt_b, w_b, w_c, a_log, skip, w_out,
          w_cam_t, w_q4, w_k4, w_v, w_bn1_t, w_bn2_t, consts, out):
    seq_d = nc.dram_tensor("seq_d", [IMAGES, CH, L], F32, kind="Internal").ap()
    x1_d = nc.dram_tensor("x1_d", [IMAGES, CH, L], F32, kind="Internal").ap()
    s1q_d = nc.dram_tensor("s1q_d", [IMAGES, P, L], BF16, kind="Internal").ap()
    t2q_d = nc.dram_tensor("t2q_d", [IMAGES, CH, L], BF16, kind="Internal").ap()
    s1k_d = nc.dram_tensor("s1k_d", [IMAGES, P, L], BF16, kind="Internal").ap()
    t2k_d = nc.dram_tensor("t2k_d", [IMAGES, CH, L], BF16, kind="Internal").ap()
    vt_d = nc.dram_tensor("vt_d", [IMAGES, P, KT, CH], F32, kind="Internal").ap()

    with ExitStack() as top:
        banks = [top.enter_context(nc.psum_tensor(f"bank{i}", [P, 512], F32)) for i in range(8)]
        convolutions(nc, banks, x, w1, b1, w2, b2, seq_d)
        pipeline(nc, banks, seq_d, (x1_d, s1q_d, t2q_d, s1k_d, t2k_d, vt_d), w_in, cw, cb, w_dt_t,
                 w_dt, dt_b, w_b, w_c, a_log, skip, w_out, w_cam_t, w_q4, w_k4, w_v, w_bn1_t,
                 w_bn2_t, consts, out)


def clear(nc, sems):
    for s in sems:
        nc.gpsimd.sem_clear(s)
    nc.all_engine_barrier()


def convolutions(nc, banks, x, w1, b1, w2, b2, seq_d):
    with ExitStack() as ctx:
        def sb(name, shape, dt=F32):
            return ctx.enter_context(nc.sbuf_tensor(name, shape, dt))

        def sem(name):
            return ctx.enter_context(nc.semaphore(name))

        wbd = [sb("w1bd", [P, 9, P]), sb("w2bd", [P, 9, P])]
        bias = sb("bias", [P, 2])
        xpad = sb("xpad", [P, PAD, PAD])
        ypad = sb("ypad", [P, PAD, PAD])
        biased = sb("biased", [P, 2, CHUNK])
        seq = sb("seq", [P, 2, CHUNK])

        zeroed, w_in_sem = sem("zeroed"), sem("conv_weights")
        with nc.Block() as block:
            @block.vector
            def _(dve):
                nc.vector.memset(wbd[0][:], 0.0).then_inc(zeroed, 1)
                nc.vector.memset(wbd[1][:], 0.0).then_inc(zeroed, 1)

            @block.gpsimd
            def _(pool):
                nc.gpsimd.memset(xpad[:], 0.0)
                nc.gpsimd.memset(ypad[:], 0.0)

            @block.sync
            def _(sp):
                sp.wait_ge(zeroed, 2)
                for bd, w, b, col in ((wbd[0], w1, b1, 0), (wbd[1], w2, b2, 1)):
                    for half in (0, CH):
                        sp.dma_start(bd[half:half + CH, :, half:half + CH], w).then_inc(w_in_sem, 16)
                        sp.dma_start(bias[half:half + CH, col:col + 1], b).then_inc(w_in_sem, 16)
                sp.wait_ge(w_in_sem, 8 * 16)
        clear(nc, [zeroed, w_in_sem])

        loaded, summed, plus_bias, leaky = (sem(n) for n in ("loaded", "summed", "plus_bias", "leaky"))
        stored = [sem("stored0"), sem("stored1")]

        def pair(p):
            with nc.Block() as block:
                @block.sync
                def _(sp):
                    src = x[bass.ds(p, 1)].rearrange("a p h w -> (a p) h w")
                    for h in range(4):
                        r = h * 16
                        sp.dma_start(xpad[:, 1 + r:17 + r, 1:1 + WW], src[:, r:r + 16, :]).then_inc(loaded, 16)
                    for k in range(CHUNKS):
                        sp.wait_ge(leaky, CHUNKS + k + 1)
                        sp.dma_start(seq_d[bass.ds(p * 2, 2)].rearrange("a c l -> (a c) l")
                                     [:, k * CHUNK:(k + 1) * CHUNK], seq[:, k % 2, :]).then_inc(stored[k % 2], 16)
                    for s in stored:
                        sp.wait_ge(s, 16 * CHUNKS // 2)

                @block.tensor
                def _(pe):
                    pe.wait_ge(loaded, 64)
                    for n in range(2 * CHUNKS):
                        conv, k = n // CHUNKS, n % CHUNKS
                        src = (xpad, ypad)[conv]
                        if n >= 8:
                            pe.wait_ge(plus_bias, n - 7)
                        if conv:
                            pe.wait_ge(leaky, min(k + 2, CHUNKS))
                        for tap in range(9):
                            dy, dx = tap // 3, tap % 3
                            mm = nc.tensor.matmul(
                                banks[n % 8][:].rearrange("p (h w) -> p h w", w=WW), wbd[conv][:, tap, :],
                                src[:, k * ROWS + dy:k * ROWS + dy + ROWS, dx:dx + WW],
                                start=tap == 0, stop=tap == 8)
                        mm.then_inc(summed, 1)

                @block.scalar
                def _(act):
                    for n in range(2 * CHUNKS):
                        conv = n // CHUNKS
                        act.wait_ge(summed, n + 1)
                        if n >= 2:
                            act.wait_ge(leaky, n - 1)
                        nc.scalar.activation(biased[:, n % 2, :], banks[n % 8][:], ACT.Identity,
                                             bias=bias[:, conv:conv + 1]).then_inc(plus_bias, 1)

                @block.vector
                def _(dve):
                    for n in range(2 * CHUNKS):
                        conv, k = n // CHUNKS, n % CHUNKS
                        dve.wait_ge(plus_bias, n + 1)
                        src = biased[:, n % 2, :]
                        if conv == 0:
                            dst = ypad[:, 1 + k * ROWS:1 + (k + 1) * ROWS, 1:1 + WW]
                            src = src.rearrange("p (h w) -> p h w", w=WW)
                        else:
                            dst = seq[:, k % 2, :]
                            if k >= 2:
                                dve.wait_ge(stored[k % 2], 16 * (k // 2))
                        nc.vector.scalar_tensor_tensor(out=dst, in0=src, scalar=LEAK, in1=src, op0=ALU.mult,
                                                       op1=ALU.max).then_inc(leaky, 1)
            clear(nc, [loaded, summed, plus_bias, leaky, *stored])

        with nc.Fori(0, PAIRS) as p:
            pair(p)


def pipeline(nc, banks, seq_d, scratch, w_in, cw, cb, w_dt_t, w_dt, dt_b, w_b, w_c, a_log, skip,
             w_out, w_cam_t, w_q4, w_k4, w_v, w_bn1_t, w_bn2_t, consts, out):
    x1_d, s1q_d, t2q_d, s1k_d, t2k_d, vt_d = scratch
    RB, (UB, ACC, DEN, YPS) = banks[0:RING], banks[RING:]
    AUX = RB[0]
    with ExitStack() as ctx:
        def sb(name, shape, dt=F32):
            return ctx.enter_context(nc.sbuf_tensor(name, shape, dt))

        def sem(name):
            return ctx.enter_context(nc.semaphore(name))

        cst = sb("cst", [P, C_END])
        selb = sb("selb", [P, GPB, P], BF16)
        win = sb("win", [P, 2 * D_INNER])
        wdt = sb("wdt", [P, D_INNER])
        wb = sb("wb", [P, P])
        wc = sb("wc", [P, P])
        wout = sb("wout", [P, CH])
        wq = sb("wq", [P, P])
        wk = sb("wk", [P, P])
        wxv = sb("wxv", [P, 2 * CH])
        wbn1 = sb("wbn1", [CH, CH])
        mixw = sb("mixw", [P, P])
        small = sb("small", [P, 8 + 2 * GROUPS])
        taps, convb, dtb, dskip = small[:, 0:4], small[:, 4:5], small[:, 5:6], small[:, 6:7]
        alog, amat = small[:, 8:8 + GROUPS], small[:, 8 + GROUPS:8 + 2 * GROUPS]
        ones = sb("ones", [P, 32])
        ident = cst[:, C_ID:C_ID + P]
        seqt = sb("seqt", [P, 2, CHUNK])
        xin = sb("xin", [P, 2, CHUNK + D_CONV - 1])
        cacc = sb("cacc", [P, CHUNK])
        u = sb("u", [P, 2, CHUNK])
        zs = sb("zs", [P, 2, CHUNK])
        bbc = sb("bbc", [P, 2, CHUNK])
        cbc = sb("cbc", [P, 2, CHUNK])
        dtx = sb("dtx", [P, CHUNK])
        em = sb("em", [P, CHUNK])
        em1 = sb("em1", [P, CHUNK])
        dsp = sb("dsp", [P, 3, CHUNK])
        usp = sb("usp", [P, 3, CHUNK])
        stk = sb("stk", [96, 2, 2, BLOCKS, CHUNK])
        dA = sb("dA", [P, 2, CHUNK])
        dbu = sb("dbu", [P, CHUNK])
        hst = sb("hst", [P, SRING, CHUNK])
        carry = sb("carry", [P, GROUPS])
        hc = sb("hc", [P, HRING, CHUNK])
        ysb = sb("ysb", [P, CHUNK])
        x1c = sb("x1c", [P, 2, CHUNK])
        full = sb("full", [P, 2, CHUNK])
        head = sb("head", [P, 2, CHUNK], BF16)
        rest = sb("rest", [CH, 2, CHUNK])
        mid = sb("mid", [CH, 2, CHUNK], BF16)
        s1st = sb("s1st", [P, 2, CHUNK], BF16)
        t2st = sb("t2st", [CH, 2, CHUNK], BF16)
        xv = sb("xv", [P, 4, 2 * CH])
        energy = sb("energy", [CH, CH])
        s1k = sb("s1k", [P, L], BF16)
        t2k = sb("t2k", [P, L], BF16)
        s1kx = sb("s1kx", [P, L], BF16)
        s1q = sb("s1q", [P, 2, QUARTER], BF16)
        t2q = sb("t2q", [P, 2, QUARTER], BF16)
        vt = sb("vt", [P, KT, CH])
        pr = sb("pr", [P, PRING, 2, CHUNK])
        x1a = sb("x1a", [P, CHUNK])
        mxp = sb("mxp", [P, NT, CHUNKS])
        mx = sb("mx", [P, NT])
        nmx = sb("nmx", [NT, 3, P])
        nm3 = sb("nm3", [NT, 3, P], BF16)
        accs = sb("accs", [P, CHUNK])
        dens = sb("dens", [P, CHUNK])
        rinv = dens
        res = sb("res", [P, CHUNK])
        catt = sb("catt", [CH, CH])
        cst1 = sb("cst1", [CH, 4])

        zeroed, got, capped, made, wps, wdone = (
            sem(n) for n in ("zeroed", "got", "capped", "made", "wps", "wdone"))
        wdtt = dA[0:DT_RANK, 0, 0:P]
        wdt4 = dA[0:DT_RANK, 1, 0:P]
        wvt = dA[0:CH, 0, P:P + CH]
        wbn2 = dA[0:CH, 1, P:P + CH]
        loads = [(cst[:], consts), (win[0:CH, :], w_in), (wb[:], w_b), (wc[:], w_c), (wout[:], w_out),
                 (wq[0:CH, :], w_q4), (wk[0:CH, :], w_k4), (wxv[0:CH, 0:CH], w_cam_t), (wbn1[:], w_bn1_t),
                 (taps, cw), (convb, cb), (dtb, dt_b), (dskip, skip), (alog, a_log),
                 (wdtt, w_dt_t), (wdt4, w_dt), (wvt, w_v), (wbn2, w_bn2_t)]
        zero = [win, wq, wk, wxv, seqt, x1c]
        with nc.Block() as block:
            @block.vector
            def _(dve):
                for t in zero:
                    nc.vector.memset(t[CH:P], 0.0)
                nc.vector.memset(mixw[:], 0.0)
                nc.vector.memset(ones[:], 1.0).then_inc(zeroed, 1)
                dve.wait_ge(got, 16 * len(loads))
                nc.vector.tensor_scalar(alog, alog, A_LOG_MAX, None, ALU.min).then_inc(capped, 1)
                nc.vector.tensor_scalar(small[:, 0:5], small[:, 0:5], 0.5, None, ALU.mult)
                nc.vector.tensor_scalar(win[0:CH, D_INNER:], win[0:CH, D_INNER:], 0.5, None, ALU.mult)

            @block.gpsimd
            def _(pool):
                nc.gpsimd.memset(t2k[CH:P, :], 0.0).then_inc(made, 1)
                nc.gpsimd.memset(t2q[CH:P, :, :], 0.0)
                pool.wait_ge(made, 1)
                nc.gpsimd.memset(t2k[CH:CH + 3, :], 1.0)

            @block.sync
            def _(sp):
                for dst, src in loads:
                    sp.dma_start(dst, src).then_inc(got, 16)
                sp.wait_ge(got, 16 * len(loads))

            @block.tensor
            def _(pe):
                pe.wait_ge(got, 16 * len(loads))
                nc.tensor.matmul(AUX[:, 0:P], wdtt, wdt4, start=True, stop=True).then_inc(wps, 1)
                nc.tensor.matmul(YPS[0:CH, 0:CH], wvt, wbn2, start=True, stop=True).then_inc(wps, 1)

            @block.scalar
            def _(act):
                act.wait_ge(got, 16 * len(loads))
                act.wait_ge(capped, 1)
                nc.scalar.copy(selb[:].rearrange("p g n -> p (g n)"), cst[:, C_SEL:C_SUM])
                nc.scalar.activation(amat, alog, ACT.Exp).then_inc(wdone, 1)
                act.wait_ge(wdone, 1)
                nc.scalar.mul(amat, amat, -1.0)
                act.wait_ge(wps, 2)
                nc.scalar.copy(wdt[:], AUX[:, 0:P])
                nc.scalar.copy(wxv[0:CH, CH:2 * CH], YPS[0:CH, 0:CH])
        clear(nc, [zeroed, got, capped, made, wps, wdone])

        names = """xin_in conv tanh gated z_gated em_in em1_in ln_in delta_in du_in dres ures seq0 seq1 stk00 stk01 stk02 stk03 stk10 stk11 stk12 stk13
                   da_in u_full dbu_in scan carried hc_in y_mm y_in y2_in st_x1 qk_in rest_in mid_in
                   t2_in abs_in  st_split st_vt ring_full act_took dve_took p_full pv den ld_kx ld_kx3 ld_k0 ld_k1 ld_k2 ld_k3
                   ld_q0 ld_q1 ld_x max_in cmax cexp catt_in nm3_in nm_row acc_in den_in st_out
                   dstep gstep""".split()
        S = {n: sem(n) for n in names}

        def step(j, i):
            sched = Step(j)
            number, now, back = sched.number, sched.now, sched.back

            def image_of(scratch, d):
                return scratch[bass.ds(i - d, 1)].rearrange(
                    "a p l -> (a p) l" if len(scratch.shape) == 3 else "a p k c -> (a p) k c")

            def wait(eng, name, event, times=1):
                value = sched.counts.get(name, {}).get(event)
                if value is not None:
                    eng.wait_ge(S[name], value * times)

            def found_rows(T):
                return sched.searches(T) and sched.searches(T)[2] == SPAN + 2

            def bank_of(e):
                return RB[number[e] % RING]

            def full_wait(eng, e):
                if e in number:
                    eng.wait_ge(S["ring_full"], number[e] + 1)

            def taken(eng, e):
                if e in sched.freed:
                    eng.wait_ge(S[sched.freed[e][0]], sched.freed[e][1])

            for T in range(sched.first, sched.last):
                sl, r = T // GROUPS, T % GROUPS
                if sched.scans(T):
                    for n in ("dbu_in", "scan", "hc_in"):
                        sched.note(n, T)
                if sched.carries(T - 1):
                    sched.note("carried", T - 1)
                c = sl + 1
                if sched.prepares(c):
                    for at, n in ((0, "xin_in"), (2, "conv"), (4, "tanh"), (5, "gated"), (6, "z_gated"), (6, "abs_in"), (6, "em_in"), (7, "em1_in"),
                                  (8, "ln_in"), (9, "delta_in"), (9, "du_in"), (9, "dres"), (10, "ures")):
                        if r == at:
                            sched.note(n, c)
                    if r in (9, 10):
                        sched.note("gstep", (c, r))
                    if r == 10:
                        for b in range(BLOCKS):
                            sched.note(f"stk{c % 2}{b}", c)
                if r == 4 and (c + 2 <= CHUNKS - 1 and now or c + 2 > CHUNKS - 1 and sched.next):
                    sched.note(f"seq{c % 2}", c + 2)
                elif T == sched.first == -GROUPS:
                    sched.note("seq0", 0)
                    sched.note("seq1", 1)
                c = sl - 1
                if sl >= 0 and sched.follows(c):
                    for at, n in ((3, "y_in"), (3, "y2_in"), (6, "st_x1"), (14, "t2_in"), (14, "st_split"), (13, "st_vt")):
                        if r == at:
                            sched.note(n, c)
                    for at, n, w in ((9, "qk_in", 0), (10, "qk_in", 1), (11, "rest_in", 0), (12, "rest_in", 1),
                                     (12, "mid_in", 0), (13, "mid_in", 1)):
                        if r == at:
                            sched.note(n, (c, w))
                found = sched.searches(T)
                if found and found[2] == SPAN - 1:
                    sched.note("max_in", found[:2])
                if found and found[2] == SPAN + 1:
                    sched.note("nm3_in", found[:2])
                if found and found[2] == SPAN + 2:
                    sched.note("nm_row", found[:2])
                if T >= 0 and sched.ended(T):
                    sched.note("acc_in", sched.ended(T))
                    sched.note("den_in", sched.ended(T))
                if T >= 8 and sched.ended(T - 8):
                    sched.note("st_out", sched.ended(T - 8))
                for q in range(QUARTERS):
                    d, at = (1, QUARTER_LOAD + KT * q)
                    if T == at and back[d]:
                        sched.note(f"ld_q{q % 2}", (d, q))
                    at = MAIN + 12 + KT * q
                    d, at = (1, at) if at < TICKS else (2, at - TICKS)
                    if T == at and back[d]:
                        sched.note("ld_x", (d, q))

            first, last = sched.first, sched.last
            with nc.Block() as block:
                @block.sync
                def _(sp):
                    def load_seq(c):
                        d, k = (0, c) if c < CHUNKS else (-1, c - CHUNKS)
                        sp.dma_start(seqt[0:CH, c % 2, :], image_of(seq_d, d)
                                     [:, k * CHUNK:(k + 1) * CHUNK]).then_inc(S[f"seq{c % 2}"], 16)

                    total = {}

                    def issued(ins, name):
                        ins.then_inc(S[name], 16)
                        total[name] = total.get(name, 0) + 16

                    if first < 0:
                        load_seq(0)
                        load_seq(1)
                    for T in range(first, last):
                        sl, r = T // GROUPS, T % GROUPS
                        c = sl + 1
                        if r == 4 and (c + 2 < CHUNKS and now or c + 2 >= CHUNKS and sched.next):
                            full_wait(sp, ("z", c))
                            load_seq(c + 2)
                        if sched.prepares(c) and r in (10, 11):
                            w = r - 10
                            if r == 10:
                                wait(sp, "u_full", (GROUPS * (c - 1) - 1,))
                                wait(sp, "dres", c)
                            else:
                                wait(sp, "ures", c)
                            src = (dsp, usp)[w]
                            for j in range(BLOCKS):
                                for s in range(3):
                                    sp.dma_start(stk[BLOCK * s:BLOCK * (s + 1), c % 2, w, j, :],
                                                 src[BLOCK * j:BLOCK * (j + 1), s, :]).then_inc(S[f"stk{c % 2}{j}"], 16)
                        c = sl - 1
                        if sl >= 0 and sched.follows(c):
                            d, k = (0, c) if c >= 0 else (1, CHUNKS - 1)
                            cols = slice(k * CHUNK, (k + 1) * CHUNK)
                            if r == 6:
                                taken(sp, ("out", c))
                                issued(sp.dma_start(image_of(x1_d, d)[:, cols], x1c[0:CH, c % 2, :]), "st_x1")
                            if r == 14:
                                wait(sp, "t2_in", c)
                                for w, (s1_d, t2_d) in enumerate(((s1q_d, t2q_d), (s1k_d, t2k_d))):
                                    issued(sp.dma_start(image_of(s1_d, d)[:, cols], s1st[:, w, :]), "st_split")
                                    issued(sp.dma_start(image_of(t2_d, d)[:, cols], t2st[:, w, :]), "st_split")
                            if r == 13:
                                taken(sp, ("xv", c))
                                issued(sp.dma_start(image_of(vt_d, d)[:, 4 * k:4 * (k + 1), :],
                                                    xv[:, :, CH:2 * CH]), "st_vt")
                        if back[1] and T == KX_LOAD:
                            full_wait(sp, ("max", (2, QUARTERS - 1), NT * CHUNKS - 1))
                            for p in range(QUARTERS - 1):
                                cols = slice(p * QUARTER, (p + 1) * QUARTER)
                                issued(sp.dma_start(s1kx[:, cols], image_of(s1k_d, 1)[:, cols]), "ld_kx")
                        if back[1] and T == GROUPS:
                            wait(sp, "st_split", -1, 64)
                            cols = slice((QUARTERS - 1) * QUARTER, L)
                            issued(sp.dma_start(s1kx[:, cols], image_of(s1k_d, 1)[:, cols]), "ld_kx3")
                        for p in range(QUARTERS):
                            cols = slice(p * QUARTER, (p + 1) * QUARTER)
                            if back[1] and T == MAIN - KT + 8 * (p + 1) + 1:
                                full_wait(sp, ("S", MAIN - KT + 8 * (p + 1) - 1, 1))
                                wait(sp, "pv", (MAIN - KT + 8 * (p + 1) - 1,))
                                if p == QUARTERS - 1:
                                    wait(sp, "st_vt", -1, 16)
                                issued(sp.dma_start(s1k[:, cols], image_of(s1k_d, 1)[:, cols]), f"ld_k{p}")
                                issued(sp.dma_start(t2k[0:CH, cols], image_of(t2k_d, 1)[:, cols]), f"ld_k{p}")
                                issued(sp.dma_start(vt[:, 8 * p:8 * (p + 1), :],
                                                    image_of(vt_d, 1)[:, 8 * p:8 * (p + 1), :]), f"ld_k{p}")
                            if back[1] and T == QUARTER_LOAD + KT * p:
                                full_wait(sp, ("S", KT * p + MAIN - KT - 1, 1))
                                issued(sp.dma_start(s1q[:, p % 2, :], image_of(s1q_d, 1)[:, cols]), f"ld_q{p % 2}")
                                issued(sp.dma_start(t2q[0:CH, p % 2, :], image_of(t2q_d, 1)[:, cols]),
                                       f"ld_q{p % 2}")
                            at = MAIN + 12 + KT * p
                            d, at = (1, at) if at < TICKS else (2, at - TICKS)
                            if back[d] and T == at:
                                full_wait(sp, ("res", (d, p - 1) if p else (2, QUARTERS - 1)))
                                for h in range(2):
                                    a = p * QUARTER + h * CHUNK
                                    issued(sp.dma_start(x1a[CH * h:CH * (h + 1), :],
                                                        image_of(x1_d, d)[:, a:a + CHUNK]), "ld_x")
                        if T >= 8 and sched.ended(T - 8):
                            d, q = sched.ended(T - 8)
                            taken(sp, ("res", (d, q)))
                            for h in range(2):
                                a = q * QUARTER + h * CHUNK
                                issued(sp.dma_start(image_of(out, d)[:, a:a + CHUNK],
                                                    res[CH * h:CH * (h + 1), :]), "st_out")
                    total["nm_row"] = 48 * len(sched.counts.get("nm_row", ()))
                    for name, value in total.items():
                        if value:
                            sp.wait_ge(S[name], value)
                    for name in ("seq0", "seq1"):
                        if name in sched.counts:
                            sp.wait_ge(S[name], 16 * len(sched.counts[name]))
                    for name in [f"stk{par}{j}" for par in range(2) for j in range(BLOCKS)]:
                        if name in sched.counts:
                            sp.wait_ge(S[name], 16 * 6 * len(sched.counts[name]))

                @block.tensor
                def _(pe):
                    def take_bank(e):
                        if number[e] >= RING:
                            taken(pe, sched.uses[number[e] - RING])
                        return bank_of(e)

                    def small_use(e):
                        kind, c = e[0], e[1]
                        bank = take_bank(e)
                        if kind == "max":
                            (d, q), k = e[1:]
                            nt, mc = k // CHUNKS, k % CHUNKS
                            if k == 0:
                                wait(pe, f"ld_q{q % 2}", (d, q), 32)
                                if (d, q) == (1, 0):
                                    pe.wait_ge(S["ld_kx"], 16 * (QUARTERS - 1))
                            if (d, q) == (1, 0) and k == 2 * (QUARTERS - 1):
                                pe.wait_ge(S["ld_kx3"], 16)
                            mm = nc.tensor.matmul(bank[:], s1q[:, q % 2, nt * P:(nt + 1) * P],
                                                  s1kx[:, mc * CHUNK:(mc + 1) * CHUNK], start=True, stop=True)
                        elif kind == "turn":
                            wait(pe, "max_in", c)
                            mm = nc.tensor.matmul(bank[0:NT, 0:P], mx[:], ident, start=True, stop=True)
                        elif kind == "mix":
                            pe.wait_ge(S["catt_in"], 1)
                            for h in (slice(0, CH), slice(CH, P)):
                                mm = nc.tensor.matmul(bank[h, 0:CH], catt[:], wbn1[:], start=True, stop=True)
                        elif kind == "den":
                            wait(pe, "den_in", c)
                            mm = nc.tensor.matmul(bank[:], cst[:, C_DEN:C_DEN + P], dens[:], start=True, stop=True)
                        elif kind == "res":
                            wait(pe, "ld_x", c, 32)
                            if c[0] == 1:
                                taken(pe, ("mix", 1))
                            mm = nc.tensor.matmul(bank[:], mixw[:], x1a[:], start=True, stop=True)
                        elif kind in ("xin", "z"):
                            wait(pe, f"seq{c % 2}", c, 16)
                            o = 0 if kind == "xin" else D_INNER
                            mm = nc.tensor.matmul(bank[:], win[:, o:o + D_INNER], seqt[:, c % 2, :],
                                                  start=True, stop=True)
                        elif kind in ("dt", "B", "C"):
                            wait(pe, "gated", c)
                            w = {"dt": wdt, "B": wb, "C": wc}[kind]
                            mm = nc.tensor.matmul(bank[:], w[:], u[:, c % 2, :], start=True, stop=True)
                        elif kind == "out":
                            wait(pe, "y2_in", c)
                            mm = nc.tensor.matmul(bank[0:CH, :], wout[:], ysb[:], start=True, stop=True)
                        elif kind in ("q", "k"):
                            taken(pe, ("out", c))
                            mm = nc.tensor.matmul(bank[:], (wq if kind == "q" else wk)[:], x1c[:, c % 2, :],
                                                  start=True, stop=True)
                        elif kind == "xv":
                            for t in range(4):
                                mm = nc.tensor.matmul(bank[:, t * P:(t + 1) * P], x1c[:, c % 2, t * P:(t + 1) * P],
                                                      wxv[:], start=True, stop=True)
                        elif kind == "en":
                            taken(pe, ("xv", c))
                            for t in range(4):
                                mm = nc.tensor.matmul(bank[0:CH, 0:CH], xv[:, t, 0:CH], xv[:, t, 0:CH],
                                                      start=t == 0, stop=t == 3)
                        mm.then_inc(S["ring_full"], 1)

                    def scores(e):
                        T, h = e[1:]
                        d, q, t = sched.attends(T)
                        if t == 0:
                            wait(pe, "nm_row", (d, q), 48)
                        if (d, q) == (1, 0) and t % 8 == 0:
                            pe.wait_ge(S[f"ld_k{t // 8}"], 16 * 3)
                        bank = take_bank(e)
                        cols = slice(h * CHUNK, (h + 1) * CHUNK)
                        nc.tensor.matmul(bank[:], s1k[:, t * P:(t + 1) * P], s1q[:, q % 2, cols],
                                         start=True, stop=False)
                        nc.tensor.matmul(bank[:], t2k[:, t * P:(t + 1) * P], t2q[:, q % 2, cols],
                                         start=False, stop=True).then_inc(S["ring_full"], 1)

                    def values(T):
                        d, q, t = sched.had(T)
                        taken(pe, ("S", T, 1))
                        if t == 0:
                            wait(pe, "acc_in", sched.ended(T))
                        for h in range(2):
                            mm = nc.tensor.matmul(ACC[CH * h:CH * (h + 1), :], vt[:, t, :],
                                                  pr[:, T % PRING, h, :], start=t == 0, stop=t == KT - 1)
                        mm.then_inc(S["pv"], 1)

                    def sums(T):
                        t = sched.had(T)[2]
                        if t == 1:
                            wait(pe, "den_in", sched.ended(T - 1))
                        for par in range(2):
                            for h in range(2):
                                o = 64 * par + 32 * h
                                mm = nc.tensor.matmul(DEN[o:o + 32, :], ones[:], pr[:, (T - 1 + par) % PRING, h, :],
                                                      start=t == 1, stop=t == KT - 1, tile_position=(0, o))
                        mm.then_inc(S["den"], 1)

                    def reduce_states(b):
                        gl = b % GPB
                        if gl == 0:
                            wait(pe, "y_in", b // GPB - 1)
                        wait(pe, "hc_in", BLOCKS * b + BLOCKS - 1)
                        for j in range(BLOCKS):
                            mm = nc.tensor.matmul(YPS[BLOCK * j:BLOCK * (j + 1), :],
                                                  cst[:, C_SUM + BLOCK * gl:C_SUM + BLOCK * (gl + 1)],
                                                  hc[:, (BLOCKS * b + j) % HRING, :],
                                                  start=gl == 0, stop=gl == GPB - 1, tile_position=(0, BLOCK * j))
                        mm.then_inc(S["y_mm"], 1)

                    def spread(T, w, bank):
                        c, g = T // GROUPS, group_of(T)
                        if T % GROUPS < BLOCKS:
                            wait(pe, f"stk{c % 2}{g // GPB}", c, 16 * 6)
                        return nc.tensor.matmul(bank[:], selb[0:96, g % GPB, :],
                                                stk[:, c % 2, w, g // GPB, :].bitcast(BF16)[:, 1::2],
                                                start=True, stop=True)

                    for T in range(first, last):
                        for e in sched.plan(T):
                            if e[0] == "S":
                                scores(e)
                            elif e[0] == "D":
                                spread(e[1], 0, take_bank(e)).then_inc(S["ring_full"], 1)
                            elif e[0] == "U":
                                wait(pe, "dbu_in", e[1] - 1)
                                spread(e[1], 1, UB).then_inc(S["u_full"], 1)
                            elif e[0] == "PV":
                                values(e[1])
                            elif e[0] == "SUM":
                                sums(e[1])
                            elif e[0] == "Y":
                                reduce_states(e[1])
                            else:
                                small_use(e)

                @block.scalar
                def _(act):
                    def small_use(e):
                        kind, c = e[0], e[1]
                        if kind in DVE_USES:
                            return
                        if kind == "xin":
                            if c % CHUNKS:
                                wait(act, "conv", c - 2)
                                taken(act, ("xin", c - 1))
                                nc.scalar.copy(xin[:, c % 2, 0:D_CONV - 1],
                                               xin[:, (c - 1) % 2, CHUNK:CHUNK + D_CONV - 1]).then_inc(
                                    S["xin_in"], 1)
                            else:
                                wait(act, "conv", c - 2)
                        elif kind == "z":
                            wait(act, "y2_in", c - 2)
                        elif kind == "dt":
                            wait(act, "delta_in", c - 1)
                        elif kind == "B":
                            wait(act, "dbu_in", GROUPS * (c - 1) - 1)
                        elif kind == "C":
                            wait(act, "hc_in", GROUPS * (c - 1) - 1)
                        elif kind == "out":
                            wait(act, "st_x1", c - 1, 16)
                        elif kind in ("q", "k"):
                            wait(act, "t2_in", c - 1)
                        elif kind == "xv":
                            taken(act, ("en", c - 1))
                            wait(act, "st_vt", c - 1, 16)
                        full_wait(act, e)
                        bank = bank_of(e)
                        w = 0 if kind == "q" else 1
                        h = 0 if kind == "den" else c % 2
                        dst, src = {
                            "xin": (xin[:, h, D_CONV - 1:], bank[:]), "z": (zs[:, h, :], bank[:]),
                            "dt": (dtx[:], bank[:]), "B": (bbc[:, h, :], bank[:]), "C": (cbc[:, h, :], bank[:]),
                            "out": (x1c[0:CH, h, :], bank[0:CH, :]), "q": (full[:, 0, :], bank[:]),
                            "k": (full[:, 1, :], bank[:]), "den": (dens[:], bank[:]), "xv": (xv[:].rearrange("p t n -> p (t n)"), bank[:])}[kind]
                        if kind == "dt":
                            nc.scalar.activation(dst, src, ACT.Identity, bias=dtb).then_inc(S["act_took"], 1)
                        else:
                            nc.scalar.copy(dst, src).then_inc(S["act_took"], 1)
                        if kind in ("q", "k"):
                            taken(act, e)
                            nc.scalar.copy(head[:, w, :], full[:, w, :]).then_inc(S["qk_in"], 1)

                    for T in range(first, last):
                        sl, r = T // GROUPS, T % GROUPS
                        if sched.attends(T):
                            wait(act, "pv", (T - PRING,))
                            wait(act, "den", ((T - PRING) // 2 * 2 + 1,))
                            for h in range(2):
                                full_wait(act, ("S", T, h))
                                nc.scalar.activation(pr[:, T % PRING, h, :], bank_of(("S", T, h))[:],
                                                     ACT.Exp).then_inc(S["p_full"], 1)
                        if sched.spreads(T + 1):
                            full_wait(act, ("D", T + 1))
                            wait(act, "scan", T - 1)
                            g = group_of(T + 1)
                            nc.scalar.activation(dA[:, (T + 1) % 2, :], bank_of(("D", T + 1))[:], ACT.Exp,
                                                 scale=amat[:, g:g + 1]).then_inc(S["da_in"], 1)
                        if sched.carries(T - 1):
                            wait(act, "scan", T - 1)
                            g = group_of(T - 1)
                            nc.scalar.copy(carry[:, g:g + 1],
                                           hst[:, (T - 1) % SRING, CHUNK - 1:CHUNK]).then_inc(S["carried"], 1)
                        for e in sched.small_uses(T):
                            small_use(e)
                        done = sched.ended(T)
                        if done:
                            taken(act, ("res", sched.before(done)))
                            wait(act, "den", (T - 1,))
                            nc.scalar.copy(dens[:], DEN[:]).then_inc(S["den_in"], 1)
                        if found_rows(T):
                            d, q = sched.searches(T)[:2]
                            wait(act, "nm3_in", (d, q))
                            if d == 1:
                                full_wait(act, ("S", KT * q + MAIN - KT - 1, 1))
                            for s in range(3):
                                act.dma_start(t2q[CH + s:CH + s + 1, q % 2, :], nm3[:, s, :]).then_inc(S["nm_row"], 16)
                        c = sl + 1
                        if sched.prepares(c) and r == 4:
                            wait(act, "conv", c)
                            wait(act, "du_in", c - 2)
                            wait(act, "delta_in", c - 1)
                            wait(act, "y_in", c - 2)
                            nc.scalar.activation(u[:, c % 2, :], cacc[:], ACT.Tanh)
                            taken(act, ("z", c))
                            nc.scalar.activation(em1[:], zs[:, c % 2, :], ACT.Tanh).then_inc(S["tanh"], 1)
                        if sched.prepares(c) and r == 6:
                            taken(act, ("dt", c))
                            wait(act, "gated", c)
                            nc.scalar.activation(em[:], dtx[:], ACT.Abs).then_inc(S["abs_in"], 1)
                            wait(act, "abs_in", c)
                            nc.scalar.activation(em[:], em[:], ACT.Exp, scale=-1.0).then_inc(S["em_in"], 1)
                        if sched.prepares(c) and r == 8:
                            wait(act, "em1_in", c)
                            nc.scalar.activation(em1[:], em1[:], ACT.Ln).then_inc(S["ln_in"], 1)
                        c = sl - 1
                        if sl >= 0 and sched.follows(c) and r in (12, 13):
                            w = r - 12
                            wait(act, "rest_in", (c, w))
                            nc.scalar.copy(mid[:, w, :], rest[:, w, :]).then_inc(S["mid_in"], 1)
                        if T == GROUPS and back[1]:
                            act.wait_ge(S["cmax"], 1)
                            nc.scalar.activation(catt[:], energy[:], ACT.Exp, bias=cst1[:, 0:1],
                                                 accum_out=cst1[:, 1:2]).then_inc(S["cexp"], 1)

                @block.vector
                def _(dve):
                    steps = [0]

                    def link(ins):
                        steps[0] += 1
                        ins.then_inc(S["dstep"], 1)
                        dve.wait_ge(S["dstep"], steps[0])

                    def small_use(e):
                        kind, c = e[0], e[1]
                        if kind not in DVE_USES:
                            return
                        full_wait(dve, e)
                        bank = bank_of(e)
                        if kind == "max":
                            (d, q), k = e[1:]
                            nc.vector.reduce_max(mxp[:, k // CHUNKS, k % CHUNKS:k % CHUNKS + 1], bank[:],
                                                 AX_X).then_inc(S["dve_took"], 1)
                            if k == NT * CHUNKS - 1:
                                taken(dve, e)
                                nc.vector.tensor_reduce(mx[:], mxp[:], AX_X, ALU.max).then_inc(S["max_in"], 1)
                        elif kind == "turn":
                            wait(dve, "nm_row", (c[0], c[1] - 1) if c[1] else (2, QUARTERS - 1), 48)
                            nc.vector.tensor_scalar(nmx[:, 0, :], bank[0:NT, 0:P], -1.0, None,
                                                    ALU.mult).then_inc(S["dve_took"], 1)
                            taken(dve, e)
                            link(nc.vector.tensor_copy(nm3[:, 0, :], nmx[:, 0, :]))
                            link(nc.vector.tensor_tensor(nmx[:, 1, :], nmx[:, 0, :], nm3[:, 0, :], ALU.subtract))
                            link(nc.vector.tensor_copy(nm3[:, 1, :], nmx[:, 1, :]))
                            nc.vector.tensor_tensor(nm3[:, 2, :], nmx[:, 1, :], nm3[:, 1, :],
                                                    ALU.subtract).then_inc(S["nm3_in"], 1)
                        elif kind == "mix":
                            nc.vector.tensor_tensor(mixw[0:CH, 0:CH], bank[0:CH, 0:CH], ident[0:CH, 0:CH], ALU.add)
                            nc.vector.tensor_tensor(mixw[CH:P, CH:P], bank[CH:P, 0:CH], ident[CH:P, CH:P],
                                                    ALU.add).then_inc(S["dve_took"], 1)
                        elif kind == "res":
                            wait(dve, "st_out", (c[0], c[1] - 1) if c[1] else (2, QUARTERS - 1), 32)
                            nc.vector.tensor_tensor(res[:], accs[:], bank[:], ALU.add).then_inc(S["dve_took"], 1)
                        elif kind == "en":
                            if c == 0:
                                ins = nc.vector.tensor_copy(energy[:], bank[0:CH, 0:CH])
                            else:
                                taken(dve, ("en", c - 1))
                                ins = nc.vector.tensor_tensor(energy[:], energy[:], bank[0:CH, 0:CH], ALU.add)
                            ins.then_inc(S["dve_took"], 1)

                    def hi(t):
                        return t.bitcast(BF16)[:, 1::2]

                    for T in range(first, last):
                        sl, r = T // GROUPS, T % GROUPS
                        ev = sched.small_uses(T)
                        c = sl - 1
                        if sl >= 0 and sched.follows(c) and r == 3:
                            wait(dve, "y_mm", (GPB * (c + 1) - 1,))
                            full_wait(dve, ("out", c - 1))
                            nc.vector.scalar_tensor_tensor(out=ysb[:], in0=u[:, c % 2, :], scalar=dskip, in1=YPS[:],
                                                           op0=ALU.mult, op1=ALU.add).then_inc(S["y_in"], 1)
                        if sched.scans(T):
                            wait(dve, "u_full", (T,))
                            if r == 0:
                                taken(dve, ("B", sl))
                            wait(dve, "scan", T - 1)
                            nc.vector.tensor_tensor(dbu[:], UB[:], bbc[:, sl % 2, :], ALU.mult).then_inc(
                                S["dbu_in"], 1)
                        if sched.scans(T):
                            g = group_of(T)
                            wait(dve, "dbu_in", T)
                            taken(dve, ("D", T))
                            wait(dve, "hc_in", T - SRING)
                            wait(dve, "carried", T - SRING)
                            nc.vector.tensor_tensor_scan(
                                hst[:, T % SRING, :], dA[:, T % 2, :], dbu[:],
                                carry[:, g:g + 1] if sl else 0.0, ALU.mult, ALU.add).then_inc(S["scan"], 1)
                        c = sl + 1
                        if sched.prepares(c):
                            x_ = xin[:, c % 2, :]
                            if r == 0 and c % CHUNKS == 0:
                                wait(dve, "conv", c - 2)
                                nc.vector.memset(xin[:, 0, 0:D_CONV - 1], 0.0).then_inc(S["xin_in"], 1)
                            if r == 1:
                                wait(dve, "xin_in", c)
                                taken(dve, ("xin", c))
                                wait(dve, "gated", c - 1)
                                link(nc.vector.tensor_scalar(cacc[:], x_[:, 0:CHUNK], taps[:, 0:1], convb,
                                                             ALU.mult, ALU.add))
                            for k in ((), (1,), (2, 3))[r] if r < 3 else ():
                                ins = nc.vector.scalar_tensor_tensor(
                                    out=cacc[:], in0=x_[:, k:k + CHUNK], scalar=taps[:, k:k + 1], in1=cacc[:],
                                    op0=ALU.mult, op1=ALU.add)
                                if k < D_CONV - 1:
                                    link(ins)
                                else:
                                    ins.then_inc(S["conv"], 1)
                            if r == 5:
                                wait(dve, "tanh", c)
                                nc.vector.scalar_tensor_tensor(out=u[:, c % 2, :], in0=u[:, c % 2, :], scalar=1.0,
                                                               in1=cacc[:], op0=ALU.add,
                                                               op1=ALU.mult).then_inc(S["gated"], 1)
                            if r == 6:
                                nc.vector.scalar_tensor_tensor(out=zs[:, c % 2, :], in0=em1[:], scalar=1.0,
                                                               in1=zs[:, c % 2, :], op0=ALU.add,
                                                               op1=ALU.mult).then_inc(S["z_gated"], 1)
                            if r == 7:
                                wait(dve, "em_in", c)
                                wait(dve, "z_gated", c)
                                link(nc.vector.tensor_scalar(em1[:], em[:], 1.0, None, ALU.add))
                                nc.vector.scalar_tensor_tensor(out=em[:], in0=em1[:], scalar=1.0, in1=em[:],
                                                               op0=ALU.subtract, op1=ALU.subtract).then_inc(
                                    S["em1_in"], 1)
                            if r == 9:
                                wait(dve, "ln_in", c)
                                link(nc.vector.tensor_tensor(em1[:], em1[:], em[:], ALU.subtract))
                                for b in range(BLOCKS):
                                    wait(dve, f"stk{(c - 1) % 2}{b}", c - 1, 16 * 6)
                                nc.vector.scalar_tensor_tensor(out=dsp[:, 0, :], in0=dtx[:], scalar=0.0, in1=em1[:],
                                                               op0=ALU.max, op1=ALU.add).then_inc(S["delta_in"], 1)
                        c = sl - 1
                        if sl >= 0 and sched.follows(c) and r in (11, 12, 14):
                            for w in range(2):
                                m1 = cst[:, C_MASK + w:C_MASK + w + 1]
                                m2 = cst[0:CH, C_MASK + 2 + w:C_MASK + 3 + w]
                                if r == 11 + w:
                                    wait(dve, "qk_in", (c, w))
                                    wait(dve, "st_split", c - 1, 64)
                                    nc.vector.scalar_tensor_tensor(
                                        out=rest[:, w, :], in0=head[0:CH, w, :], scalar=m2, in1=full[0:CH, w, :],
                                        op0=ALU.mult, op1=ALU.add).then_inc(S["rest_in"], 1)
                                    nc.vector.scalar_tensor_tensor(
                                        out=s1st[:, w, :], in0=head[:, w, :], scalar=m1, in1=full[:, w, :],
                                        op0=ALU.mult, op1=ALU.add)
                                if r == 14:
                                    wait(dve, "mid_in", (c, w))
                                    ins = nc.vector.scalar_tensor_tensor(
                                        out=t2st[:, w, :], in0=mid[:, w, :], scalar=m2, in1=rest[:, w, :],
                                        op0=ALU.mult, op1=ALU.add)
                                    if w:
                                        ins.then_inc(S["t2_in"], 1)
                        done = sched.ended(T)
                        if done:
                            taken(dve, ("res", sched.before(done)))
                            wait(dve, "pv", (T - 1,))
                            nc.vector.tensor_copy(accs[:], ACC[:]).then_inc(S["acc_in"], 1)
                        for part in range(4):
                            done = T >= 3 + part and sched.ended(T - 3 - part)
                            if done:
                                cols = slice(part * P, (part + 1) * P)
                                taken(dve, ("den", done))
                                link(nc.vector.reciprocal(rinv[:, cols], dens[:, cols]))
                                if part == 3:
                                    link(nc.vector.tensor_tensor(accs[:], accs[:], rinv[:], ALU.mult))
                        for e in ev:
                            small_use(e)
                        if T == GROUPS and back[1]:
                            taken(dve, ("en", -1))
                            nc.vector.tensor_reduce(cst1[:, 0:1], energy[:], AX_X, ALU.max,
                                                    negate=True).then_inc(S["cmax"], 1)
                            dve.wait_ge(S["cexp"], 1)
                            link(nc.vector.reciprocal(cst1[:, 2:3], cst1[:, 1:2]))
                            nc.vector.tensor_scalar(catt[:], catt[:], cst1[:, 2:3], None, ALU.mult).then_inc(
                                S["catt_in"], 1)

                @block.gpsimd
                def _(pool):
                    def hi(t):
                        return t.bitcast(BF16)[:, 1::2]

                    for T in range(first, last):
                        sl, r = T // GROUPS, T % GROUPS
                        if sched.scans(T):
                            if r == 0:
                                taken(pool, ("C", sl))
                            wait(pool, "scan", T)
                            wait(pool, "y_mm", ((T - HRING) // BLOCKS,))
                            nc.gpsimd.tensor_tensor(hc[:, T % HRING, :], hst[:, T % SRING, :], cbc[:, sl % 2, :],
                                                    ALU.mult).then_inc(S["hc_in"], 1)
                        c = sl - 1
                        if sl >= 0 and sched.follows(c) and r == 3:
                            wait(pool, "y_in", c)
                            wait(pool, "z_gated", c)
                            nc.gpsimd.tensor_tensor(ysb[:], ysb[:], zs[:, c % 2, :], ALU.mult).then_inc(
                                S["y2_in"], 1)
                        c = sl + 1
                        if sched.prepares(c) and r in (9, 10):
                            t, name = ((dsp, "dres"), (usp, "ures"))[r - 9]
                            if r == 9:
                                wait(pool, "delta_in", c)
                            else:
                                wait(pool, "du_in", c)
                            nc.gpsimd.tensor_tensor(t[:, 1, :], t[:, 0, :], hi(t[:, 0, :]),
                                                    ALU.subtract).then_inc(S["gstep"], 1)
                            wait(pool, "gstep", (c, r))
                            nc.gpsimd.tensor_tensor(t[:, 2, :], t[:, 1, :], hi(t[:, 1, :]),
                                                    ALU.subtract).then_inc(S[name], 1)
                            if r == 9:
                                nc.gpsimd.tensor_tensor(usp[:, 0, :], dsp[:, 0, :], u[:, c % 2, :],
                                                        ALU.mult).then_inc(S["du_in"], 1)
            clear(nc, list(S.values()))

        step(0, 0)
        step(1, 1)
        with nc.Fori(2, IMAGES - 1) as i:
            step(2, i)
        step(IMAGES - 1, IMAGES - 1)
        step(IMAGES, IMAGES)
        step(IMAGES + 1, IMAGES + 1)


def kernel(x, L0_conv_conv_w1, L0_conv_conv_b1, L0_conv_conv_w2, L0_conv_conv_b2, L0_conv_in_proj_w,
           L0_conv_conv1d_w, L0_conv_conv1d_b, L0_conv_x_proj_w, L0_conv_dt_proj_w, L0_conv_dt_proj_b,
           L0_conv_A_log, L0_conv_D, L0_conv_out_proj_w, L1_conv_w_cam, L1_conv_w_q, L1_conv_w_k,
           L1_conv_w_v, L1_conv_w_bn):
    import numpy as np
    import concourse.bacc as bacc
    from concourse.bass_utils import run_bass_kernel_spmd

    def taps_first(w):
        return np.asarray(w).reshape(CH, CH, 9).transpose(1, 2, 0)

    def lanes(w):
        return np.repeat(np.asarray(w), DL, axis=1)

    col = lambda v: np.asarray(v).reshape(-1, 1)
    xp = np.asarray(L0_conv_x_proj_w)
    bn = np.asarray(L1_conv_w_bn)
    arrays = dict(
        x=np.asarray(x).reshape(PAIRS, P, HH, WW),
        w1=taps_first(L0_conv_conv_w1), b1=col(L0_conv_conv_b1),
        w2=taps_first(L0_conv_conv_w2), b2=col(L0_conv_conv_b2),
        w_in=np.asarray(L0_conv_in_proj_w),
        cw=np.asarray(L0_conv_conv1d_w).reshape(D_INNER, D_CONV), cb=col(L0_conv_conv1d_b),
        w_dt_t=xp[:, 0:DT_RANK].T, w_dt=np.asarray(L0_conv_dt_proj_w), dt_b=col(L0_conv_dt_proj_b),
        w_b=lanes(xp[:, DT_RANK:DT_RANK + D_STATE]), w_c=lanes(xp[:, DT_RANK + D_STATE:]),
        a_log=np.asarray(L0_conv_A_log).reshape(GROUPS, DL, D_STATE).transpose(2, 1, 0).reshape(P, GROUPS),
        skip=col(L0_conv_D), w_out=np.asarray(L0_conv_out_proj_w),
        w_cam_t=np.asarray(L1_conv_w_cam).T,
        w_q4=np.tile(np.asarray(L1_conv_w_q).T, (1, 4)), w_k4=np.tile(np.asarray(L1_conv_w_k).T, (1, 4)),
        w_v=np.asarray(L1_conv_w_v), w_bn1_t=bn[:, 0:CH].T, w_bn2_t=bn[:, CH:].T,
        consts=shape_constants())
    nc = bacc.Bacc("TRN2", target_bir_lowering=False, num_devices=1)
    given, args = {}, {}
    for name, a in arrays.items():
        a = np.ascontiguousarray(a)
        given[f"in_{name}"] = a
        args[name] = nc.dram_tensor(f"in_{name}", a.shape, mybir.dt.from_np(a.dtype), kind="ExternalInput").ap()
    out = nc.dram_tensor("out_0", (IMAGES, CH, L), F32, kind="ExternalOutput").ap()
    build(nc, out=out, **args)
    r = run_bass_kernel_spmd(nc, [given], core_ids=[0])
    return r.results[0]["out_0"].reshape(IMAGES, CH, HH, WW)
```

```python
from contextlib import ExitStack

import concourse.bass as bass
from concourse import mybir

F32 = mybir.dt.float32
BF16 = mybir.dt.bfloat16
ALU = mybir.AluOpType
ACT = mybir.ActivationFunctionType
AX_X = mybir.AxisListType.X

P = 128
IMAGES, CH, HH, WW = 16, 64, 64, 64
L = HH * WW
PAIRS = IMAGES // 2
PAD = HH + 2
D_INNER, D_STATE, D_CONV, DT_RANK = 128, 16, 4, 4
LEAK = 0.01
A_LOG_MAX = 84.0
CHUNK = 512
CHUNKS = L // CHUNK
ROWS = CHUNK // WW
DL = P // D_STATE
GROUPS = D_INNER // DL
BLOCK = 32
BLOCKS = D_INNER // BLOCK
GPB = BLOCK // DL
QDIM = CH // 2
QUARTER = 1024
QUARTERS = L // QUARTER
KT = L // P
NT = QUARTER // P
TICKS = CHUNKS * GROUPS
assert TICKS == QUARTERS * KT
MAIN = 48
SEARCH = 18
QUARTER_LOAD = 16
KX_LOAD = 13
SPAN = 26
END = 14
PRING = 4
HRING = 8
BATCH = 4

C_ID = 0
C_SEL = C_ID + P
C_SUM = C_SEL + GPB * P
C_DEN = C_SUM + GPB * BLOCK
C_MASK = C_DEN + P
C_END = C_MASK + 2


THREES = [GROUPS + r for r in (4, 6, 8, 9, 14)] + [2 * GROUPS + r for r in (0, 4, 5, 8, 9, 10, 11)]
TRIED = [0]
for t in range(SPAN):
    TRIED.append(min(NT * CHUNKS, TRIED[t] + (3 if SEARCH + t in THREES else 2)))
assert TRIED[SPAN] == NT * CHUNKS


def shape_constants():
    import numpy as np
    c = np.zeros((P, C_END), np.float32)
    c[:, C_ID:C_ID + P] = np.eye(P)
    for lane in range(P):
        for g in range(GPB):
            row = DL * g + lane % DL
            for s in range(3):
                c[BLOCK * s + row, C_SEL + P * g + lane] = 1
            c[lane, C_SUM + BLOCK * g + row] = 1
    for col in range(P):
        half = col // CH
        c[32 * half, C_DEN + col] = 1
        c[64 + 32 * half, C_DEN + col] = 1
    block = np.arange(P) // 32
    c[:, C_MASK] = -1.0 * ((block == 1) | (block == 3))
    c[:, C_MASK + 1] = -1.0 * ((block == 0) | (block == 3))
    return c


def group_of(T):
    k = T % GROUPS
    return k % BLOCKS * GPB + k // BLOCKS


class Step:

    def __init__(self, j):
        self.now, self.next = 0 <= j < IMAGES, 0 <= j + 1 < IMAGES
        self.back = {d: 0 <= j - d < IMAGES for d in (1, 2)}
        self.first = -GROUPS if j == 0 else 0
        self.last = TICKS if j <= IMAGES else MAIN + END + 1
        self.uses, self.number, self.freed = [], {}, {}
        self.counts = {}
        for T in range(self.first, self.last):
            for e in self.plan(T):
                if e[0] in SIGNAL_OF:
                    self.note(SIGNAL_OF[e[0]], e[1:])
                    continue
                self.number[e] = len(self.uses)
                self.uses.append(e)
                signal = {"S": "p_full", "D": "da_in"}.get(e[0], "dve_took" if e[0] in DVE_USES else "act_took")
                self.freed[e] = (signal, self.note(signal, e))

    def note(self, name, event):
        c = self.counts.setdefault(name, {})
        c[event] = len(c) + 1
        return len(c)

    def prepares(self, c):
        return c < CHUNKS and self.now or c == CHUNKS and self.next

    def follows(self, c):
        return self.now if c >= 0 else self.back[1]

    def scans(self, T):
        return self.now and 0 <= T < TICKS

    def carries(self, T):
        return self.scans(T) and T < TICKS - GROUPS

    def scanned(self, T):
        return self.scans(T) and T < TICKS - 1 or T == -1 and self.back[1]

    def spreads(self, T):
        return T >= 0 and T > self.first and self.prepares(T // GROUPS)

    def attends(self, T):
        d, lin = (1, T - MAIN) if T >= MAIN else (2, T - MAIN + TICKS)
        return (d, lin // KT, lin % KT) if self.back[d] and lin >= 0 and T < TICKS else None

    def ended(self, T):
        d, lin = (1, T - MAIN) if T > MAIN else (2, T - MAIN + TICKS)
        return (d, lin // KT - 1) if self.back[d] and lin % KT == 0 and lin >= KT else None

    @staticmethod
    def before(quarter):
        d, q = quarter
        return (d, q - 1) if q else (d + 1, QUARTERS - 1)

    def searches(self, T):
        d, lin = (1, T - SEARCH) if T >= SEARCH else (2, T - SEARCH + TICKS)
        return (d, lin // KT, lin % KT) if self.back[d] and lin >= 0 and T >= 0 else None

    def small_uses(self, T):
        ev = []
        found = self.searches(T)
        if found:
            d, q, t = found
            if t < SPAN:
                ev += [("max", (d, q), k) for k in range(TRIED[t], TRIED[t + 1])]
            if t == SPAN + 1:
                ev.append(("turn", (d, q)))
        if T == MAIN + 14 and self.back[1]:
            ev.append(("mix", 1))
        for lag, name in ((3, "den"), (13, "res")):
            done = self.ended(T - lag)
            if done and T - lag >= 0:
                ev.append((name, done))
        sl, r = T // GROUPS, T % GROUPS
        name = {0: "xin", 5: "z", 6: "dt", 11: "C", 14: "B"}.get(r)
        if name and self.prepares(sl + 1):
            ev.append((name, sl + 1))
        name = {7: "out", 9: "q", 10: "k", 12: "xv", 14: "en"}.get(r)
        if name and sl >= 0 and self.follows(sl - 1):
            ev.append((name, sl - 1))
        return ev

    def plan(self, T):
        uses, plan = self.small_uses(T), []
        if self.attends(T):
            plan += [("S", T, 0), ("S", T, 1)]
        if self.spreads(T + 1):
            plan.append(("D", T + 1))
        if T >= 0 and self.had(T - 1):
            plan.append(("PV", T - 1))
        plan += uses[0:1]
        if self.spreads(T + 1):
            plan.append(("U", T + 1))
        b = T // BATCH - 1
        if T >= 0 and T % BATCH == 1 and self.had(T - 2):
            plan.append(("SUM", b))
        if T >= 0 and T % BATCH == BATCH - 1 and (self.back[1] if b < 0 else self.now):
            plan.append(("Y", b))
        return plan + uses[1:]

    def had(self, T):
        return self.attends(T) if T >= 0 else (2, (TICKS - MAIN - 1) // KT, (TICKS - MAIN - 1) % KT) \
            if self.back[2] else None


SIGNAL_OF = {"PV": "pv", "U": "u_full", "SUM": "den", "Y": "y_mm"}
DVE_USES = ("max", "turn", "mix", "res", "en")
RING = 4


def build(nc, x, w1, b1, w2, b2, w_in, cw, cb, w_dt_t, w_dt, dt_b, w_b, w_c, a_log, skip, w_out,
          w_cam_t, w_q4, w_k4, w_v, w_bn1_t, w_bn2_t, consts, out):
    seq_d = nc.dram_tensor("seq_d", [IMAGES, CH, L], F32, kind="Internal").ap()
    x1_d = nc.dram_tensor("x1_d", [IMAGES, CH, L], F32, kind="Internal").ap()
    s1q_d = nc.dram_tensor("s1q_d", [IMAGES, P, L], BF16, kind="Internal").ap()
    t2q_d = nc.dram_tensor("t2q_d", [IMAGES, CH, L], BF16, kind="Internal").ap()
    s1k_d = nc.dram_tensor("s1k_d", [IMAGES, P, L], BF16, kind="Internal").ap()
    t2k_d = nc.dram_tensor("t2k_d", [IMAGES, CH, L], BF16, kind="Internal").ap()
    vt_d = nc.dram_tensor("vt_d", [IMAGES, P, KT, CH], F32, kind="Internal").ap()

    with ExitStack() as top:
        banks = [top.enter_context(nc.psum_tensor(f"bank{i}", [P, 512], F32)) for i in range(8)]
        convolutions(nc, banks, x, w1, b1, w2, b2, seq_d)
        pipeline(nc, banks, seq_d, (x1_d, s1q_d, t2q_d, s1k_d, t2k_d, vt_d), w_in, cw, cb, w_dt_t,
                 w_dt, dt_b, w_b, w_c, a_log, skip, w_out, w_cam_t, w_q4, w_k4, w_v, w_bn1_t,
                 w_bn2_t, consts, out)


ROWS_OF = (0, 10, 26, 42, HH)
NEEDS = {10: 0, 18: 1, 34: 2, 50: 3}
PASSES = 6


def clear(nc, sems):
    for s in sems:
        nc.gpsimd.sem_clear(s)
    nc.all_engine_barrier()


def convolutions(nc, banks, x, w1, b1, w2, b2, seq_d):
    with ExitStack() as ctx:
        def sb(name, shape, dt=F32):
            return ctx.enter_context(nc.sbuf_tensor(name, shape, dt))

        def sem(name):
            return ctx.enter_context(nc.semaphore(name))

        wtap = [sb("w1tap", [P, PASSES, CH]), sb("w2tap", [P, PASSES, CH])]
        bias = sb("bias", [P, 2])
        xpad = [sb(f"xpad{i}", [P, PAD, PAD]) for i in range(2)]
        ypad = [sb(f"ypad{i}", [P, PAD, PAD]) for i in range(2)]
        biased = sb("biased", [P, 2, CHUNK])
        seq = sb("seq", [P, 2, CHUNK])

        w_in_sem = sem("conv_weights")
        with nc.Block() as block:
            @block.vector
            def _(dve):
                nc.vector.memset(wtap[0][CH:P, 3:6, :], 0.0)
                nc.vector.memset(wtap[1][CH:P, 3:6, :], 0.0)

            @block.gpsimd
            def _(pool):
                for t in xpad + ypad:
                    nc.gpsimd.memset(t[:], 0.0)

            @block.sync
            def _(sp):
                for t, w, b, col in ((wtap[0], w1, b1, 0), (wtap[1], w2, b2, 1)):
                    sp.dma_start(t[0:CH, 0:3, :], w[:, 0:3, :]).then_inc(w_in_sem, 16)
                    sp.dma_start(t[CH:P, 0:3, :], w[:, 3:6, :]).then_inc(w_in_sem, 16)
                    sp.dma_start(t[0:CH, 3:6, :], w[:, 6:9, :]).then_inc(w_in_sem, 16)
                    for half in (0, CH):
                        sp.dma_start(bias[half:half + CH, col:col + 1], b).then_inc(w_in_sem, 16)
                sp.wait_ge(w_in_sem, 10 * 16)
        clear(nc, [w_in_sem])

        summed, plus_bias, leaky = (sem(n) for n in ("summed", "plus_bias", "leaky"))
        loaded = [sem(f"loaded{h}") for h in range(4)]
        moved = [sem(f"moved{k}") for k in range(CHUNKS)]
        stored = [sem("stored0"), sem("stored1")]

        def pair(p):
            with nc.Block() as block:
                @block.sync
                def _(sp):
                    src = x[bass.ds(p, 1)].rearrange("a p h w -> (a p) h w")
                    for h in range(4):
                        a, b = ROWS_OF[h:h + 2]
                        for i in range(2):
                            img = src[CH * i:CH * (i + 1), a:b, :]
                            sp.dma_start(xpad[i][0:CH, 1 + a:1 + b, 1:1 + WW], img).then_inc(loaded[h], 16)
                            sp.dma_start(xpad[i][CH:P, a:b, 1:1 + WW], img).then_inc(loaded[h], 16)
                    for k in range(CHUNKS):
                        sp.wait_ge(leaky, k + 1)
                        low, high = slice(1 + k * ROWS, 1 + (k + 1) * ROWS), slice(k * ROWS, (k + 1) * ROWS)
                        sp.dma_start(ypad[0][CH:P, high, 1:1 + WW],
                                     ypad[0][0:CH, low, 1:1 + WW]).then_inc(moved[k], 16)
                        sp.dma_start(ypad[1][0:CH, low, 1:1 + WW],
                                     ypad[1][CH:P, high, 1:1 + WW]).then_inc(moved[k], 16)
                    for k in range(CHUNKS):
                        sp.wait_ge(leaky, CHUNKS + k + 1)
                        sp.dma_start(seq_d[bass.ds(p * 2, 2)].rearrange("a c l -> (a c) l")
                                     [:, k * CHUNK:(k + 1) * CHUNK], seq[:, k % 2, :]).then_inc(stored[k % 2], 16)
                    for s in stored:
                        sp.wait_ge(s, 16 * CHUNKS // 2)

                @block.tensor
                def _(pe):
                    for n in range(2 * CHUNKS):
                        conv, k = n // CHUNKS, n % CHUNKS
                        src = (xpad, ypad)[conv]
                        if n >= 8:
                            pe.wait_ge(plus_bias, n - 7)
                        if conv:
                            for near in ({0, 1} if k == 0 else {min(k + 1, CHUNKS - 1)}):
                                pe.wait_ge(moved[near], 32)
                        elif k * ROWS + ROWS + 2 in NEEDS:
                            pe.wait_ge(loaded[NEEDS[k * ROWS + ROWS + 2]], 64)
                        for t in range(PASSES):
                            dy, dx = t // 3 * 2, t % 3
                            for i in range(2):
                                mm = nc.tensor.matmul(
                                    banks[n % 8][CH * i:CH * (i + 1), :].rearrange("p (h w) -> p h w", w=WW),
                                    wtap[conv][:, t, :], src[i][:, k * ROWS + dy:k * ROWS + dy + ROWS, dx:dx + WW],
                                    start=t == 0, stop=t == PASSES - 1)
                        mm.then_inc(summed, 1)

                @block.scalar
                def _(act):
                    for n in range(2 * CHUNKS):
                        conv = n // CHUNKS
                        act.wait_ge(summed, n + 1)
                        if n >= 2:
                            act.wait_ge(leaky, n - 1)
                        nc.scalar.activation(biased[:, n % 2, :], banks[n % 8][:], ACT.Identity,
                                             bias=bias[:, conv:conv + 1]).then_inc(plus_bias, 1)

                @block.vector
                def _(dve):
                    for n in range(2 * CHUNKS):
                        conv, k = n // CHUNKS, n % CHUNKS
                        dve.wait_ge(plus_bias, n + 1)
                        src = biased[:, n % 2, :]
                        if conv == 0:
                            src = src.rearrange("p (h w) -> p h w", w=WW)
                            nc.vector.scalar_tensor_tensor(
                                out=ypad[0][0:CH, 1 + k * ROWS:1 + (k + 1) * ROWS, 1:1 + WW], in0=src[0:CH],
                                scalar=LEAK, in1=src[0:CH], op0=ALU.mult, op1=ALU.max)
                            nc.vector.scalar_tensor_tensor(
                                out=ypad[1][CH:P, k * ROWS:(k + 1) * ROWS, 1:1 + WW], in0=src[CH:P],
                                scalar=LEAK, in1=src[CH:P], op0=ALU.mult, op1=ALU.max).then_inc(leaky, 1)
                        else:
                            if k >= 2:
                                dve.wait_ge(stored[k % 2], 16 * (k // 2))
                            nc.vector.scalar_tensor_tensor(out=seq[:, k % 2, :], in0=src, scalar=LEAK, in1=src,
                                                           op0=ALU.mult, op1=ALU.max).then_inc(leaky, 1)
            clear(nc, [*loaded, *moved, summed, plus_bias, leaky, *stored])

        with nc.Fori(0, PAIRS) as p:
            pair(p)


def pipeline(nc, banks, seq_d, scratch, w_in, cw, cb, w_dt_t, w_dt, dt_b, w_b, w_c, a_log, skip,
             w_out, w_cam_t, w_q4, w_k4, w_v, w_bn1_t, w_bn2_t, consts, out):
    x1_d, s1q_d, t2q_d, s1k_d, t2k_d, vt_d = scratch
    RB, (UB, ACC, DEN, YPS) = banks[0:RING], banks[RING:]
    AUX = RB[0]
    with ExitStack() as ctx:
        def sb(name, shape, dt=F32):
            return ctx.enter_context(nc.sbuf_tensor(name, shape, dt))

        def sem(name):
            return ctx.enter_context(nc.semaphore(name))

        cst = sb("cst", [P, C_END])
        selb = sb("selb", [P, GPB, P], BF16)
        win = sb("win", [P, 2 * D_INNER])
        wdt = sb("wdt", [P, D_INNER])
        wb = sb("wb", [P, P])
        wc = sb("wc", [P, P])
        wout = sb("wout", [P, CH])
        wq = sb("wq", [P, P])
        wk = sb("wk", [P, P])
        wxv = sb("wxv", [P, 2 * CH])
        wbn1 = sb("wbn1", [CH, CH])
        mixw = sb("mixw", [P, P])
        small = sb("small", [P, 8 + 2 * GROUPS])
        taps, convb, dtb, dskip = small[:, 0:4], small[:, 4:5], small[:, 5:6], small[:, 6:7]
        alog, amat = small[:, 8:8 + GROUPS], small[:, 8 + GROUPS:8 + 2 * GROUPS]
        ones = sb("ones", [P, 32])
        ident = cst[:, C_ID:C_ID + P]
        seqt = sb("seqt", [P, 2, CHUNK])
        xin = sb("xin", [P, 2, CHUNK + D_CONV - 1])
        cacc = sb("cacc", [P, CHUNK])
        u = sb("u", [P, 2, CHUNK])
        zs = sb("zs", [P, 2, CHUNK])
        bbc = sb("bbc", [P, 2, CHUNK])
        cbc = sb("cbc", [P, 2, CHUNK])
        dtx = sb("dtx", [P, CHUNK])
        em = sb("em", [P, CHUNK])
        em1 = sb("em1", [P, CHUNK])
        dsp = sb("dsp", [P, 3, CHUNK])
        usp = sb("usp", [P, 3, CHUNK])
        stk = sb("stk", [96, 2, 2, BLOCKS, CHUNK])
        dA = sb("dA", [P, 2, CHUNK])
        dbu = sb("dbu", [P, CHUNK])
        hst = sb("hst", [P, HRING, CHUNK])
        carry = sb("carry", [P, GROUPS])
        ysb = sb("ysb", [P, CHUNK])
        x1c = sb("x1c", [P, 2, CHUNK])
        full = sb("full", [P, 2, CHUNK])
        head = sb("head", [P, 2, CHUNK], BF16)
        rest = sb("rest", [P, 2, CHUNK])
        mid = sb("mid", [P, 2, CHUNK], BF16)
        t2st = sb("t2st", [CH, 2, CHUNK], BF16)
        xv = sb("xv", [P, 4, 2 * CH])
        energy = sb("energy", [CH, CH])
        s1k = sb("s1k", [P, L], BF16)
        t2k = sb("t2k", [P, L], BF16)
        s1kx = sb("s1kx", [P, L], BF16)
        s1q = sb("s1q", [P, 2, QUARTER], BF16)
        t2q = sb("t2q", [P, 2, QUARTER], BF16)
        vt = sb("vt", [P, KT, CH])
        pr = sb("pr", [P, PRING, 2, CHUNK])
        prs = sb("prs", [P, 2, 2, CHUNK])
        x1a = sb("x1a", [P, CHUNK])
        mxp = sb("mxp", [P, NT, CHUNKS])
        mx = sb("mx", [P, NT])
        nmx = sb("nmx", [NT, 3, P])
        nm3 = sb("nm3", [NT, 3, P], BF16)
        accs = sb("accs", [P, CHUNK])
        dens = sb("dens", [P, CHUNK])
        rinv = dens
        catt = sb("catt", [CH, CH])
        cst1 = sb("cst1", [CH, 4])

        zeroed, got, capped, made, wps, wdone = (
            sem(n) for n in ("zeroed", "got", "capped", "made", "wps", "wdone"))
        wdtt = dA[0:DT_RANK, 0, 0:P]
        wdt4 = dA[0:DT_RANK, 1, 0:P]
        wvt = dA[0:CH, 0, P:P + CH]
        wbn2 = dA[0:CH, 1, P:P + CH]
        loads = [(cst[:], consts), (win[0:CH, :], w_in), (wb[:], w_b), (wc[:], w_c), (wout[:], w_out),
                 (wq[0:CH, :], w_q4), (wk[0:CH, :], w_k4), (wxv[0:CH, 0:CH], w_cam_t), (wbn1[:], w_bn1_t),
                 (taps, cw), (convb, cb), (dtb, dt_b), (dskip, skip), (alog, a_log),
                 (wdtt, w_dt_t), (wdt4, w_dt), (wvt, w_v), (wbn2, w_bn2_t)]
        zero = [win, wq, wk, wxv, seqt, x1c]
        with nc.Block() as block:
            @block.vector
            def _(dve):
                for t in zero:
                    nc.vector.memset(t[CH:P], 0.0)
                nc.vector.memset(mixw[:], 0.0)
                nc.vector.memset(ones[:], 1.0).then_inc(zeroed, 1)
                dve.wait_ge(got, 16 * len(loads))
                nc.vector.tensor_scalar(alog, alog, A_LOG_MAX, None, ALU.min).then_inc(capped, 1)
                nc.vector.tensor_scalar(small[:, 0:5], small[:, 0:5], 0.5, None, ALU.mult)
                nc.vector.tensor_scalar(win[0:CH, D_INNER:], win[0:CH, D_INNER:], 0.5, None, ALU.mult)

            @block.gpsimd
            def _(pool):
                nc.gpsimd.memset(t2k[CH:P, :], 0.0).then_inc(made, 1)
                nc.gpsimd.memset(t2q[CH:P, :, :], 0.0)
                pool.wait_ge(made, 1)
                nc.gpsimd.memset(t2k[CH:CH + 3, :], 1.0)

            @block.sync
            def _(sp):
                for dst, src in loads:
                    sp.dma_start(dst, src).then_inc(got, 16)
                sp.wait_ge(got, 16 * len(loads))

            @block.tensor
            def _(pe):
                pe.wait_ge(got, 16 * len(loads))
                nc.tensor.matmul(AUX[:, 0:P], wdtt, wdt4, start=True, stop=True).then_inc(wps, 1)
                nc.tensor.matmul(YPS[0:CH, 0:CH], wvt, wbn2, start=True, stop=True).then_inc(wps, 1)

            @block.scalar
            def _(act):
                act.wait_ge(got, 16 * len(loads))
                act.wait_ge(capped, 1)
                nc.scalar.copy(selb[:].rearrange("p g n -> p (g n)"), cst[:, C_SEL:C_SUM])
                nc.scalar.activation(amat, alog, ACT.Exp).then_inc(wdone, 1)
                act.wait_ge(wdone, 1)
                nc.scalar.mul(amat, amat, -1.0)
                act.wait_ge(wps, 2)
                nc.scalar.copy(wdt[:], AUX[:, 0:P])
                nc.scalar.copy(wxv[0:CH, CH:2 * CH], YPS[0:CH, 0:CH])
        clear(nc, [zeroed, got, capped, made, wps, wdone])

        names = """xin_in conv tap_in tanh z_tanh gated z_gated em_in em1_in ln_in delta_in du_in dres ures
                   seq0 seq1 stk00 stk01 stk02 stk03 stk10 stk11 stk12 stk13 da_in u_full
                   dbu_in scan carried hc_in added y_mm y_in y2_in st_x1 qk_in rest_in
                   mid_in t2_in abs_in st_split st_vt ring_full act_took dve_took p_full
                   pv den ld_kx ld_kx3 ld_k0 ld_k1 ld_k2 ld_k3 ld_q0 ld_q1 ld_x max_in
                   cmax cexp catt_in nm3_in nm_row acc_in den_in st_out dstep gstep""".split()
        S = {n: sem(n) for n in names}

        def step(j, i):
            sched = Step(j)
            number, now, back = sched.number, sched.now, sched.back

            def image_of(scratch, d):
                return scratch[bass.ds(i - d, 1)].rearrange(
                    "a p l -> (a p) l" if len(scratch.shape) == 3 else "a p k c -> (a p) k c")

            def wait(eng, name, event, times=1):
                value = sched.counts.get(name, {}).get(event)
                if value is not None:
                    eng.wait_ge(S[name], value * times)

            def found_rows(T):
                return sched.searches(T) and sched.searches(T)[2] == SPAN + 2

            def bank_of(e):
                return RB[number[e] % RING]

            def full_wait(eng, e):
                if e in number:
                    eng.wait_ge(S["ring_full"], number[e] + 1)

            def taken(eng, e):
                if e in sched.freed:
                    eng.wait_ge(S[sched.freed[e][0]], sched.freed[e][1])

            for T in range(sched.first, sched.last):
                sl, r = T // GROUPS, T % GROUPS
                if sched.scans(T):
                    for n in ("dbu_in", "scan"):
                        sched.note(n, T)
                if sched.scanned(T - 1):
                    sched.note("hc_in", T - 1)
                if T >= 0 and T % 2 == 0 and sched.had(T - 1):
                    sched.note("added", T // 2 - 1)
                if sched.carries(T - 1):
                    sched.note("carried", T - 1)
                c = sl + 1
                if sched.prepares(c):
                    for at, n in ((0, "xin_in"), (0, "tap_in"), (3, "conv"), (4, "tanh"), (5, "z_tanh"), (5, "gated"),
                                  (6, "z_gated"), (6, "abs_in"), (6, "em_in"), (7, "em1_in"),
                                  (8, "ln_in"), (9, "delta_in"), (9, "du_in"), (9, "dres"), (10, "ures")):
                        if r == at:
                            sched.note(n, c)
                    if r in (9, 10):
                        sched.note("gstep", (c, r))
                    if r == 10:
                        for b in range(BLOCKS):
                            sched.note(f"stk{c % 2}{b}", c)
                if r == 6 and (c + 2 <= CHUNKS - 1 and now or c + 2 > CHUNKS - 1 and sched.next):
                    sched.note(f"seq{c % 2}", c + 2)
                elif T == sched.first == -GROUPS:
                    sched.note("seq0", 0)
                    sched.note("seq1", 1)
                c = sl - 1
                if sl >= 0 and sched.follows(c):
                    for at, n in ((4, "y_in"), (4, "y2_in"), (8, "st_x1"), (14, "st_split"), (13, "st_vt")):
                        if r == at:
                            sched.note(n, c)
                    for at, n, w in ((9, "qk_in", 0), (10, "qk_in", 1), (11, "rest_in", 0), (12, "rest_in", 1),
                                     (12, "mid_in", 0), (13, "mid_in", 1), (13, "t2_in", 0), (14, "t2_in", 1)):
                        if r == at:
                            sched.note(n, (c, w))
                found = sched.searches(T)
                if found and found[2] == SPAN - 1:
                    sched.note("max_in", found[:2])
                if found and found[2] == SPAN + 1:
                    sched.note("nm3_in", found[:2])
                if found and found[2] == SPAN + 2:
                    sched.note("nm_row", found[:2])
                if T >= 0 and sched.ended(T):
                    sched.note("acc_in", sched.ended(T))
                if T >= 2 and sched.ended(T - 2):
                    sched.note("den_in", sched.ended(T - 2))
                if T >= 14 and sched.ended(T - 14):
                    sched.note("st_out", sched.ended(T - 14))
                for q in range(QUARTERS):
                    d, at = (1, QUARTER_LOAD + KT * q)
                    if T == at and back[d]:
                        sched.note(f"ld_q{q % 2}", (d, q))
                    at = MAIN + 15 + KT * q
                    d, at = (1, at) if at < TICKS else (2, at - TICKS)
                    if T == at and back[d]:
                        sched.note("ld_x", (d, q))

            first, last = sched.first, sched.last
            with nc.Block() as block:
                @block.sync
                def _(sp):
                    def load_seq(c):
                        d, k = (0, c) if c < CHUNKS else (-1, c - CHUNKS)
                        sp.dma_start(seqt[0:CH, c % 2, :], image_of(seq_d, d)
                                     [:, k * CHUNK:(k + 1) * CHUNK]).then_inc(S[f"seq{c % 2}"], 16)

                    total = {}

                    def issued(ins, name):
                        ins.then_inc(S[name], 16)
                        total[name] = total.get(name, 0) + 16

                    if first < 0:
                        load_seq(0)
                        load_seq(1)
                    for T in range(first, last):
                        sl, r = T // GROUPS, T % GROUPS
                        c = sl + 1
                        if r == 6 and (c + 2 < CHUNKS and now or c + 2 >= CHUNKS and sched.next):
                            full_wait(sp, ("z", c))
                            load_seq(c + 2)
                        if sched.prepares(c) and r in (10, 11):
                            w = r - 10
                            if r == 10:
                                wait(sp, "u_full", (GROUPS * (c - 1) - 1,))
                                wait(sp, "dres", c)
                            else:
                                wait(sp, "ures", c)
                            src = (dsp, usp)[w]
                            for j in range(BLOCKS):
                                for s in range(3):
                                    sp.dma_start(stk[BLOCK * s:BLOCK * (s + 1), c % 2, w, j, :],
                                                 src[BLOCK * j:BLOCK * (j + 1), s, :]).then_inc(S[f"stk{c % 2}{j}"], 16)
                        c = sl - 1
                        if sl >= 0 and sched.follows(c):
                            d, k = (0, c) if c >= 0 else (1, CHUNKS - 1)
                            cols = slice(k * CHUNK, (k + 1) * CHUNK)
                            if r == 8:
                                taken(sp, ("out", c))
                                issued(sp.dma_start(image_of(x1_d, d)[:, cols], x1c[0:CH, c % 2, :]), "st_x1")
                            if r == 14:
                                wait(sp, "t2_in", (c, 1))
                                for w, (s1_d, t2_d) in enumerate(((s1q_d, t2q_d), (s1k_d, t2k_d))):
                                    issued(sp.dma_start(image_of(s1_d, d)[:, cols], mid[:, w, :]), "st_split")
                                    issued(sp.dma_start(image_of(t2_d, d)[:, cols], t2st[:, w, :]), "st_split")
                            if r == 13:
                                taken(sp, ("xv", c))
                                issued(sp.dma_start(image_of(vt_d, d)[:, 4 * k:4 * (k + 1), :],
                                                    xv[:, :, CH:2 * CH]), "st_vt")
                        if back[1] and T == KX_LOAD:
                            full_wait(sp, ("max", (2, QUARTERS - 1), NT * CHUNKS - 1))
                            for p in range(QUARTERS - 1):
                                cols = slice(p * QUARTER, (p + 1) * QUARTER)
                                issued(sp.dma_start(s1kx[:, cols], image_of(s1k_d, 1)[:, cols]), "ld_kx")
                        if back[1] and T == GROUPS:
                            wait(sp, "st_split", -1, 64)
                            cols = slice((QUARTERS - 1) * QUARTER, L)
                            issued(sp.dma_start(s1kx[:, cols], image_of(s1k_d, 1)[:, cols]), "ld_kx3")
                        for p in range(QUARTERS):
                            cols = slice(p * QUARTER, (p + 1) * QUARTER)
                            if back[1] and T == MAIN - KT + 8 * (p + 1) + 1:
                                full_wait(sp, ("S", MAIN - KT + 8 * (p + 1) - 1, 1))
                                wait(sp, "pv", (MAIN - KT + 8 * (p + 1) - 1,))
                                if p == QUARTERS - 1:
                                    wait(sp, "st_vt", -1, 16)
                                issued(sp.dma_start(s1k[:, cols], image_of(s1k_d, 1)[:, cols]), f"ld_k{p}")
                                issued(sp.dma_start(t2k[0:CH, cols], image_of(t2k_d, 1)[:, cols]), f"ld_k{p}")
                                issued(sp.dma_start(vt[:, 8 * p:8 * (p + 1), :],
                                                    image_of(vt_d, 1)[:, 8 * p:8 * (p + 1), :]), f"ld_k{p}")
                            if back[1] and T == QUARTER_LOAD + KT * p:
                                full_wait(sp, ("S", KT * p + MAIN - KT - 1, 1))
                                issued(sp.dma_start(s1q[:, p % 2, :], image_of(s1q_d, 1)[:, cols]), f"ld_q{p % 2}")
                                issued(sp.dma_start(t2q[0:CH, p % 2, :], image_of(t2q_d, 1)[:, cols]),
                                       f"ld_q{p % 2}")
                            at = MAIN + 15 + KT * p
                            d, at = (1, at) if at < TICKS else (2, at - TICKS)
                            if back[d] and T == at:
                                full_wait(sp, ("res", (d, p - 1) if p else (2, QUARTERS - 1)))
                                for h in range(2):
                                    a = p * QUARTER + h * CHUNK
                                    issued(sp.dma_start(x1a[CH * h:CH * (h + 1), :],
                                                        image_of(x1_d, d)[:, a:a + CHUNK]), "ld_x")
                        if T >= 14 and sched.ended(T - 14):
                            d, q = sched.ended(T - 14)
                            taken(sp, ("res", (d, q)))
                            for h in range(2):
                                a = q * QUARTER + h * CHUNK
                                issued(sp.dma_start(image_of(out, d)[:, a:a + CHUNK],
                                                    accs[CH * h:CH * (h + 1), :]), "st_out")
                    total["nm_row"] = 48 * len(sched.counts.get("nm_row", ()))
                    for name, value in total.items():
                        if value:
                            sp.wait_ge(S[name], value)
                    for name in ("seq0", "seq1"):
                        if name in sched.counts:
                            sp.wait_ge(S[name], 16 * len(sched.counts[name]))
                    for name in [f"stk{par}{j}" for par in range(2) for j in range(BLOCKS)]:
                        if name in sched.counts:
                            sp.wait_ge(S[name], 16 * 6 * len(sched.counts[name]))

                @block.tensor
                def _(pe):
                    def take_bank(e):
                        if number[e] >= RING:
                            taken(pe, sched.uses[number[e] - RING])
                        return bank_of(e)

                    def small_use(e):
                        kind, c = e[0], e[1]
                        bank = take_bank(e)
                        if kind == "max":
                            (d, q), k = e[1:]
                            nt, mc = k // CHUNKS, k % CHUNKS
                            if k == 0:
                                wait(pe, f"ld_q{q % 2}", (d, q), 32)
                                if (d, q) == (1, 0):
                                    pe.wait_ge(S["ld_kx"], 16 * (QUARTERS - 1))
                            if (d, q) == (1, 0) and k == 2 * (QUARTERS - 1):
                                pe.wait_ge(S["ld_kx3"], 16)
                            mm = nc.tensor.matmul(bank[:], s1q[:, q % 2, nt * P:(nt + 1) * P],
                                                  s1kx[:, mc * CHUNK:(mc + 1) * CHUNK], start=True, stop=True)
                        elif kind == "turn":
                            wait(pe, "max_in", c)
                            mm = nc.tensor.matmul(bank[0:NT, 0:P], mx[:], ident, start=True, stop=True)
                        elif kind == "mix":
                            pe.wait_ge(S["catt_in"], 1)
                            for h in (slice(0, CH), slice(CH, P)):
                                mm = nc.tensor.matmul(bank[h, 0:CH], catt[:], wbn1[:], start=True, stop=True)
                        elif kind == "den":
                            wait(pe, "den_in", c)
                            mm = nc.tensor.matmul(bank[:], cst[:, C_DEN:C_DEN + P], dens[:], start=True, stop=True)
                        elif kind == "res":
                            wait(pe, "ld_x", c, 32)
                            if c[0] == 1:
                                taken(pe, ("mix", 1))
                            mm = nc.tensor.matmul(bank[:], mixw[:], x1a[:], start=True, stop=True)
                        elif kind in ("xin", "z"):
                            wait(pe, f"seq{c % 2}", c, 16)
                            o = 0 if kind == "xin" else D_INNER
                            mm = nc.tensor.matmul(bank[:], win[:, o:o + D_INNER], seqt[:, c % 2, :],
                                                  start=True, stop=True)
                        elif kind in ("dt", "B", "C"):
                            wait(pe, "gated", c)
                            w = {"dt": wdt, "B": wb, "C": wc}[kind]
                            mm = nc.tensor.matmul(bank[:], w[:], u[:, c % 2, :], start=True, stop=True)
                        elif kind == "out":
                            wait(pe, "y2_in", c)
                            mm = nc.tensor.matmul(bank[0:CH, :], wout[:], ysb[:], start=True, stop=True)
                        elif kind in ("q", "k"):
                            taken(pe, ("out", c))
                            mm = nc.tensor.matmul(bank[:], (wq if kind == "q" else wk)[:], x1c[:, c % 2, :],
                                                  start=True, stop=True)
                        elif kind == "xv":
                            for t in range(4):
                                mm = nc.tensor.matmul(bank[:, t * P:(t + 1) * P], x1c[:, c % 2, t * P:(t + 1) * P],
                                                      wxv[:], start=True, stop=True)
                        elif kind == "en":
                            taken(pe, ("xv", c))
                            for t in range(4):
                                mm = nc.tensor.matmul(bank[0:CH, 0:CH], xv[:, t, 0:CH], xv[:, t, 0:CH],
                                                      start=t == 0, stop=t == 3)
                        mm.then_inc(S["ring_full"], 1)

                    def scores(e):
                        T, h = e[1:]
                        d, q, t = sched.attends(T)
                        if t == 0:
                            wait(pe, "nm_row", (d, q), 48)
                        if (d, q) == (1, 0) and t % 8 == 0:
                            pe.wait_ge(S[f"ld_k{t // 8}"], 16 * 3)
                        bank = take_bank(e)
                        cols = slice(h * CHUNK, (h + 1) * CHUNK)
                        nc.tensor.matmul(bank[:], s1k[:, t * P:(t + 1) * P], s1q[:, q % 2, cols],
                                         start=True, stop=False)
                        nc.tensor.matmul(bank[:], t2k[:, t * P:(t + 1) * P], t2q[:, q % 2, cols],
                                         start=False, stop=True).then_inc(S["ring_full"], 1)

                    def values(T):
                        d, q, t = sched.had(T)
                        taken(pe, ("S", T, 1))
                        if t == 0:
                            wait(pe, "acc_in", sched.ended(T))
                        for h in range(2):
                            mm = nc.tensor.matmul(ACC[CH * h:CH * (h + 1), :], vt[:, t, :],
                                                  pr[:, T % PRING, h, :], start=t == 0, stop=t == KT - 1)
                        mm.then_inc(S["pv"], 1)

                    def sums(b):
                        d, q, t = sched.had(BATCH * b + BATCH - 1)
                        if t == BATCH - 1:
                            wait(pe, "den_in", sched.before((d, q)))
                        wait(pe, "added", 2 * b + 1)
                        for par in range(2):
                            for h in range(2):
                                o = 64 * par + 32 * h
                                mm = nc.tensor.matmul(DEN[o:o + 32, :], ones[:], prs[:, par, h, :],
                                                      start=t == BATCH - 1, stop=t == KT - 1, tile_position=(0, o))
                        mm.then_inc(S["den"], 1)

                    def reduce_states(b):
                        gl = b % GPB
                        if gl == 0:
                            wait(pe, "y_in", b // GPB - 1)
                        wait(pe, "hc_in", BLOCKS * b + BLOCKS - 1)
                        for j in range(BLOCKS):
                            mm = nc.tensor.matmul(YPS[BLOCK * j:BLOCK * (j + 1), :],
                                                  cst[:, C_SUM + BLOCK * gl:C_SUM + BLOCK * (gl + 1)],
                                                  hst[:, (BLOCKS * b + j) % HRING, :],
                                                  start=gl == 0, stop=gl == GPB - 1, tile_position=(0, BLOCK * j))
                        mm.then_inc(S["y_mm"], 1)

                    def spread(T, w, bank):
                        c, g = T // GROUPS, group_of(T)
                        if T % GROUPS < BLOCKS:
                            wait(pe, f"stk{c % 2}{g // GPB}", c, 16 * 6)
                        return nc.tensor.matmul(bank[:], selb[0:96, g % GPB, :],
                                                stk[:, c % 2, w, g // GPB, :].bitcast(BF16)[:, 1::2],
                                                start=True, stop=True)

                    for T in range(first, last):
                        for e in sched.plan(T):
                            if e[0] == "S":
                                scores(e)
                            elif e[0] == "D":
                                spread(e[1], 0, take_bank(e)).then_inc(S["ring_full"], 1)
                            elif e[0] == "U":
                                wait(pe, "dbu_in", e[1] - 1)
                                spread(e[1], 1, UB).then_inc(S["u_full"], 1)
                            elif e[0] == "PV":
                                values(e[1])
                            elif e[0] == "SUM":
                                sums(e[1])
                            elif e[0] == "Y":
                                reduce_states(e[1])
                            else:
                                small_use(e)

                @block.scalar
                def _(act):
                    def small_use(e):
                        kind, c = e[0], e[1]
                        if kind in DVE_USES:
                            return
                        if kind == "xin":
                            if c % CHUNKS:
                                wait(act, "conv", c - 2)
                                taken(act, ("xin", c - 1))
                                nc.scalar.copy(xin[:, c % 2, 0:D_CONV - 1],
                                               xin[:, (c - 1) % 2, CHUNK:CHUNK + D_CONV - 1]).then_inc(
                                    S["xin_in"], 1)
                            else:
                                wait(act, "conv", c - 2)
                        elif kind == "z":
                            wait(act, "y2_in", c - 2)
                        elif kind == "dt":
                            wait(act, "delta_in", c - 1)
                        elif kind == "B":
                            wait(act, "dbu_in", GROUPS * (c - 1) - 1)
                        elif kind == "C":
                            wait(act, "hc_in", GROUPS * (c - 1) - 1)
                        elif kind == "out":
                            wait(act, "st_x1", c - 1, 16)
                        elif kind in ("q", "k"):
                            wait(act, "t2_in", (c - 1, 1))
                        elif kind == "xv":
                            taken(act, ("en", c - 1))
                            wait(act, "st_vt", c - 1, 16)
                        full_wait(act, e)
                        bank = bank_of(e)
                        w = 0 if kind == "q" else 1
                        h = 0 if kind == "den" else c % 2
                        dst, src = {
                            "xin": (xin[:, h, D_CONV - 1:], bank[:]), "z": (zs[:, h, :], bank[:]),
                            "dt": (dtx[:], bank[:]), "B": (bbc[:, h, :], bank[:]), "C": (cbc[:, h, :], bank[:]),
                            "out": (x1c[0:CH, h, :], bank[0:CH, :]), "q": (full[:, 0, :], bank[:]),
                            "k": (full[:, 1, :], bank[:]), "den": (dens[:], bank[:]),
                            "xv": (xv[:].rearrange("p t n -> p (t n)"), bank[:])}[kind]
                        if kind == "dt":
                            nc.scalar.activation(dst, src, ACT.Identity, bias=dtb).then_inc(S["act_took"], 1)
                        else:
                            nc.scalar.copy(dst, src).then_inc(S["act_took"], 1)
                        if kind in ("q", "k"):
                            taken(act, e)
                            nc.scalar.copy(head[:, w, :], full[:, w, :]).then_inc(S["qk_in"], 1)

                    for T in range(first, last):
                        sl, r = T // GROUPS, T % GROUPS
                        if sched.attends(T):
                            wait(act, "pv", (T - PRING,))
                            wait(act, "added", (T - PRING) // 2)
                            for h in range(2):
                                full_wait(act, ("S", T, h))
                                nc.scalar.activation(pr[:, T % PRING, h, :], bank_of(("S", T, h))[:],
                                                     ACT.Exp).then_inc(S["p_full"], 1)
                        if sched.spreads(T + 1):
                            full_wait(act, ("D", T + 1))
                            wait(act, "scan", T - 1)
                            g = group_of(T + 1)
                            nc.scalar.activation(dA[:, (T + 1) % 2, :], bank_of(("D", T + 1))[:], ACT.Exp,
                                                 scale=amat[:, g:g + 1]).then_inc(S["da_in"], 1)
                        if sched.carries(T - 1):
                            wait(act, "scan", T - 1)
                            g = group_of(T - 1)
                            nc.scalar.copy(carry[:, g:g + 1],
                                           hst[:, (T - 1) % HRING, CHUNK - 1:CHUNK]).then_inc(S["carried"], 1)
                        for e in sched.small_uses(T):
                            small_use(e)
                        done = T >= 2 and sched.ended(T - 2)
                        if done:
                            taken(act, ("res", sched.before(done)))
                            wait(act, "den", ((T - 2) // BATCH - 1,))
                            nc.scalar.copy(dens[:], DEN[:]).then_inc(S["den_in"], 1)
                        if found_rows(T):
                            d, q = sched.searches(T)[:2]
                            wait(act, "nm3_in", (d, q))
                            if d == 1:
                                full_wait(act, ("S", KT * q + MAIN - KT - 1, 1))
                            for s in range(3):
                                act.dma_start(t2q[CH + s:CH + s + 1, q % 2, :], nm3[:, s, :]).then_inc(
                                    S["nm_row"], 16)
                        c = sl + 1
                        if sched.prepares(c) and r == 0:
                            wait(act, "xin_in", c)
                            wait(act, "gated", c - 1)
                            taken(act, ("xin", c))
                            nc.scalar.activation(cacc[:], xin[:, c % 2, 0:CHUNK], ACT.Identity, bias=convb,
                                                 scale=taps[:, 0:1]).then_inc(S["tap_in"], 1)
                        if sched.prepares(c) and r == 4:
                            wait(act, "conv", c)
                            wait(act, "du_in", c - 2)
                            wait(act, "delta_in", c - 1)
                            wait(act, "y_in", c - 2)
                            nc.scalar.activation(u[:, c % 2, :], cacc[:], ACT.Tanh).then_inc(S["tanh"], 1)
                        if sched.prepares(c) and r == 5:
                            taken(act, ("z", c))
                            nc.scalar.activation(em1[:], zs[:, c % 2, :], ACT.Tanh).then_inc(S["z_tanh"], 1)
                        if sched.prepares(c) and r == 6:
                            taken(act, ("dt", c))
                            wait(act, "gated", c)
                            nc.scalar.activation(em[:], dtx[:], ACT.Abs).then_inc(S["abs_in"], 1)
                            wait(act, "abs_in", c)
                            nc.scalar.activation(em[:], em[:], ACT.Exp, scale=-1.0).then_inc(S["em_in"], 1)
                        if sched.prepares(c) and r == 8:
                            wait(act, "em1_in", c)
                            nc.scalar.activation(em1[:], em1[:], ACT.Ln).then_inc(S["ln_in"], 1)
                        c = sl - 1
                        if sl >= 0 and sched.follows(c) and r in (12, 13):
                            w = r - 12
                            wait(act, "rest_in", (c, w))
                            wait(act, "st_split", c - 1, 64)
                            nc.scalar.copy(mid[:, w, :], rest[:, w, :]).then_inc(S["mid_in"], 1)
                        if T == GROUPS and back[1]:
                            act.wait_ge(S["cmax"], 1)
                            nc.scalar.activation(catt[:], energy[:], ACT.Exp, bias=cst1[:, 0:1],
                                                 accum_out=cst1[:, 1:2]).then_inc(S["cexp"], 1)

                @block.vector
                def _(dve):
                    steps = [0]

                    def link(ins):
                        steps[0] += 1
                        ins.then_inc(S["dstep"], 1)
                        dve.wait_ge(S["dstep"], steps[0])

                    def small_use(e):
                        kind, c = e[0], e[1]
                        if kind not in DVE_USES:
                            return
                        full_wait(dve, e)
                        bank = bank_of(e)
                        if kind == "max":
                            (d, q), k = e[1:]
                            nc.vector.reduce_max(mxp[:, k // CHUNKS, k % CHUNKS:k % CHUNKS + 1], bank[:],
                                                 AX_X).then_inc(S["dve_took"], 1)
                            if k == NT * CHUNKS - 1:
                                taken(dve, e)
                                nc.vector.tensor_reduce(mx[:], mxp[:], AX_X, ALU.max).then_inc(S["max_in"], 1)
                        elif kind == "turn":
                            wait(dve, "nm_row", (c[0], c[1] - 1) if c[1] else (2, QUARTERS - 1), 48)
                            nc.vector.tensor_scalar(nmx[:, 0, :], bank[0:NT, 0:P], -1.0, None,
                                                    ALU.mult).then_inc(S["dve_took"], 1)
                            taken(dve, e)
                            link(nc.vector.tensor_copy(nm3[:, 0, :], nmx[:, 0, :]))
                            link(nc.vector.tensor_tensor(nmx[:, 1, :], nmx[:, 0, :], nm3[:, 0, :], ALU.subtract))
                            link(nc.vector.tensor_copy(nm3[:, 1, :], nmx[:, 1, :]))
                            nc.vector.tensor_tensor(nm3[:, 2, :], nmx[:, 1, :], nm3[:, 1, :],
                                                    ALU.subtract).then_inc(S["nm3_in"], 1)
                        elif kind == "mix":
                            nc.vector.tensor_tensor(mixw[0:CH, 0:CH], bank[0:CH, 0:CH], ident[0:CH, 0:CH], ALU.add)
                            nc.vector.tensor_tensor(mixw[CH:P, CH:P], bank[CH:P, 0:CH], ident[CH:P, CH:P],
                                                    ALU.add).then_inc(S["dve_took"], 1)
                        elif kind == "res":
                            nc.vector.tensor_tensor(accs[:], accs[:], bank[:], ALU.add).then_inc(S["dve_took"], 1)
                        elif kind == "en":
                            if c == 0:
                                ins = nc.vector.tensor_copy(energy[:], bank[0:CH, 0:CH])
                            else:
                                taken(dve, ("en", c - 1))
                                ins = nc.vector.tensor_tensor(energy[:], energy[:], bank[0:CH, 0:CH], ALU.add)
                            ins.then_inc(S["dve_took"], 1)

                    for T in range(first, last):
                        sl, r = T // GROUPS, T % GROUPS
                        ev = sched.small_uses(T)
                        c = sl - 1
                        if sl >= 0 and sched.follows(c) and r == 4:
                            wait(dve, "y_mm", (GPB * (c + 1) - 1,))
                            full_wait(dve, ("out", c - 1))
                            nc.vector.scalar_tensor_tensor(out=ysb[:], in0=u[:, c % 2, :], scalar=dskip, in1=YPS[:],
                                                           op0=ALU.mult, op1=ALU.add).then_inc(S["y_in"], 1)
                        if sched.scans(T):
                            wait(dve, "u_full", (T,))
                            if r == 0:
                                taken(dve, ("B", sl))
                            wait(dve, "scan", T - 1)
                            nc.vector.tensor_tensor(dbu[:], UB[:], bbc[:, sl % 2, :], ALU.mult).then_inc(
                                S["dbu_in"], 1)
                        if sched.scans(T):
                            g = group_of(T)
                            wait(dve, "dbu_in", T)
                            taken(dve, ("D", T))
                            wait(dve, "y_mm", ((T - HRING) // BATCH,))
                            nc.vector.tensor_tensor_scan(
                                hst[:, T % HRING, :], dA[:, T % 2, :], dbu[:],
                                carry[:, g:g + 1] if sl else 0.0, ALU.mult, ALU.add).then_inc(S["scan"], 1)
                        c = sl + 1
                        if sched.prepares(c):
                            x_ = xin[:, c % 2, :]
                            if r == 0 and c % CHUNKS == 0:
                                wait(dve, "conv", c - 2)
                                nc.vector.memset(xin[:, 0, 0:D_CONV - 1], 0.0).then_inc(S["xin_in"], 1)
                            if r == 1:
                                wait(dve, "xin_in", c)
                                taken(dve, ("xin", c))
                                wait(dve, "gated", c - 1)
                                wait(dve, "tap_in", c)
                            if 1 <= r < D_CONV:
                                ins = nc.vector.scalar_tensor_tensor(
                                    out=cacc[:], in0=x_[:, r:r + CHUNK], scalar=taps[:, r:r + 1], in1=cacc[:],
                                    op0=ALU.mult, op1=ALU.add)
                                if r < D_CONV - 1:
                                    link(ins)
                                else:
                                    ins.then_inc(S["conv"], 1)
                            if r == 5:
                                wait(dve, "tanh", c)
                                nc.vector.scalar_tensor_tensor(out=u[:, c % 2, :], in0=u[:, c % 2, :], scalar=1.0,
                                                               in1=cacc[:], op0=ALU.add,
                                                               op1=ALU.mult).then_inc(S["gated"], 1)
                            if r == 6:
                                wait(dve, "z_tanh", c)
                                nc.vector.scalar_tensor_tensor(out=zs[:, c % 2, :], in0=em1[:], scalar=1.0,
                                                               in1=zs[:, c % 2, :], op0=ALU.add,
                                                               op1=ALU.mult).then_inc(S["z_gated"], 1)
                            if r == 7:
                                wait(dve, "em_in", c)
                                wait(dve, "z_gated", c)
                                link(nc.vector.tensor_scalar(em1[:], em[:], 1.0, None, ALU.add))
                                nc.vector.scalar_tensor_tensor(out=em[:], in0=em1[:], scalar=1.0, in1=em[:],
                                                               op0=ALU.subtract, op1=ALU.subtract).then_inc(
                                    S["em1_in"], 1)
                            if r == 9:
                                wait(dve, "ln_in", c)
                                link(nc.vector.tensor_tensor(em1[:], em1[:], em[:], ALU.subtract))
                                for b in range(BLOCKS):
                                    wait(dve, f"stk{(c - 1) % 2}{b}", c - 1, 16 * 6)
                                nc.vector.scalar_tensor_tensor(out=dsp[:, 0, :], in0=dtx[:], scalar=0.0, in1=em1[:],
                                                               op0=ALU.max, op1=ALU.add).then_inc(S["delta_in"], 1)
                        c = sl - 1
                        if sl >= 0 and sched.follows(c) and r in (11, 12, 13, 14):
                            w = (r - 11) % 2
                            mask = cst[:, C_MASK + w:C_MASK + w + 1]
                            if r < 13:
                                wait(dve, "qk_in", (c, w))
                                nc.vector.scalar_tensor_tensor(
                                    out=rest[:, w, :], in0=head[:, w, :], scalar=mask, in1=full[:, w, :],
                                    op0=ALU.mult, op1=ALU.add).then_inc(S["rest_in"], 1)
                            else:
                                wait(dve, "mid_in", (c, w))
                                wait(dve, "st_split", c - 1, 64)
                                nc.vector.scalar_tensor_tensor(
                                    out=t2st[:, w, :], in0=mid[0:CH, w, :], scalar=mask[0:CH], in1=rest[0:CH, w, :],
                                    op0=ALU.mult, op1=ALU.add).then_inc(S["t2_in"], 1)
                        done = sched.ended(T)
                        if done:
                            wait(dve, "st_out", sched.before(done), 32)
                            wait(dve, "pv", (T - 1,))
                            nc.vector.tensor_copy(accs[:], ACC[:]).then_inc(S["acc_in"], 1)
                        for part, lag in enumerate((4, 5, 8, 10)):
                            done = T >= lag and sched.ended(T - lag)
                            if done:
                                cols = slice(part * P, (part + 1) * P)
                                taken(dve, ("den", done))
                                link(nc.vector.reciprocal(rinv[:, cols], dens[:, cols]))
                                if part == 3:
                                    link(nc.vector.tensor_tensor(accs[:], accs[:], rinv[:], ALU.mult))
                        for e in ev:
                            small_use(e)
                        if T == GROUPS and back[1]:
                            taken(dve, ("en", -1))
                            nc.vector.tensor_reduce(cst1[:, 0:1], energy[:], AX_X, ALU.max,
                                                    negate=True).then_inc(S["cmax"], 1)
                            dve.wait_ge(S["cexp"], 1)
                            link(nc.vector.reciprocal(cst1[:, 2:3], cst1[:, 1:2]))
                            nc.vector.tensor_scalar(catt[:], catt[:], cst1[:, 2:3], None, ALU.mult).then_inc(
                                S["catt_in"], 1)

                @block.gpsimd
                def _(pool):
                    def hi(t):
                        return t.bitcast(BF16)[:, 1::2]

                    for T in range(first, last):
                        sl, r = T // GROUPS, T % GROUPS
                        if T >= 0 and T % 2 == 0 and sched.had(T - 1):
                            pair = T // 2 - 1
                            taken(pool, ("S", T - 1, 1))
                            wait(pool, "den", ((pair - 2) // 2,))
                            nc.gpsimd.tensor_tensor(prs[:, pair % 2], pr[:, (T - 2) % PRING], pr[:, (T - 1) % PRING],
                                                    ALU.add).then_inc(S["added"], 1)
                        if sched.scanned(T - 1):
                            if r == 1:
                                taken(pool, ("C", sl))
                            wait(pool, "scan", T - 1)
                            wait(pool, "carried", T - 1)
                            h = hst[:, (T - 1) % HRING, :]
                            nc.gpsimd.tensor_tensor(h, h, cbc[:, (T - 1) // GROUPS % 2, :],
                                                    ALU.mult).then_inc(S["hc_in"], 1)
                        c = sl - 1
                        if sl >= 0 and sched.follows(c) and r == 4:
                            wait(pool, "y_in", c)
                            wait(pool, "z_gated", c)
                            nc.gpsimd.tensor_tensor(ysb[:], ysb[:], zs[:, c % 2, :], ALU.mult).then_inc(
                                S["y2_in"], 1)
                        c = sl + 1
                        if sched.prepares(c) and r in (9, 10):
                            t, name = ((dsp, "dres"), (usp, "ures"))[r - 9]
                            if r == 9:
                                wait(pool, "delta_in", c)
                            else:
                                wait(pool, "du_in", c)
                            nc.gpsimd.tensor_tensor(t[:, 1, :], t[:, 0, :], hi(t[:, 0, :]),
                                                    ALU.subtract).then_inc(S["gstep"], 1)
                            wait(pool, "gstep", (c, r))
                            nc.gpsimd.tensor_tensor(t[:, 2, :], t[:, 1, :], hi(t[:, 1, :]),
                                                    ALU.subtract).then_inc(S[name], 1)
                            if r == 9:
                                nc.gpsimd.tensor_tensor(usp[:, 0, :], dsp[:, 0, :], u[:, c % 2, :],
                                                        ALU.mult).then_inc(S["du_in"], 1)
            clear(nc, list(S.values()))

        step(0, 0)
        step(1, 1)
        with nc.Fori(2, IMAGES - 1) as i:
            step(2, i)
        step(IMAGES - 1, IMAGES - 1)
        step(IMAGES, IMAGES)
        step(IMAGES + 1, IMAGES + 1)


def kernel(x, L0_conv_conv_w1, L0_conv_conv_b1, L0_conv_conv_w2, L0_conv_conv_b2, L0_conv_in_proj_w,
           L0_conv_conv1d_w, L0_conv_conv1d_b, L0_conv_x_proj_w, L0_conv_dt_proj_w, L0_conv_dt_proj_b,
           L0_conv_A_log, L0_conv_D, L0_conv_out_proj_w, L1_conv_w_cam, L1_conv_w_q, L1_conv_w_k,
           L1_conv_w_v, L1_conv_w_bn):
    import numpy as np
    import concourse.bacc as bacc
    from concourse.bass_utils import run_bass_kernel_spmd

    def taps_first(w):
        return np.asarray(w).reshape(CH, CH, 9).transpose(1, 2, 0)

    def lanes(w):
        return np.repeat(np.asarray(w), DL, axis=1)

    col = lambda v: np.asarray(v).reshape(-1, 1)
    xp = np.asarray(L0_conv_x_proj_w)
    bn = np.asarray(L1_conv_w_bn)
    arrays = dict(
        x=np.asarray(x).reshape(PAIRS, P, HH, WW),
        w1=taps_first(L0_conv_conv_w1), b1=col(L0_conv_conv_b1),
        w2=taps_first(L0_conv_conv_w2), b2=col(L0_conv_conv_b2),
        w_in=np.asarray(L0_conv_in_proj_w),
        cw=np.asarray(L0_conv_conv1d_w).reshape(D_INNER, D_CONV), cb=col(L0_conv_conv1d_b),
        w_dt_t=xp[:, 0:DT_RANK].T, w_dt=np.asarray(L0_conv_dt_proj_w), dt_b=col(L0_conv_dt_proj_b),
        w_b=lanes(xp[:, DT_RANK:DT_RANK + D_STATE]), w_c=lanes(xp[:, DT_RANK + D_STATE:]),
        a_log=np.asarray(L0_conv_A_log).reshape(GROUPS, DL, D_STATE).transpose(2, 1, 0).reshape(P, GROUPS),
        skip=col(L0_conv_D), w_out=np.asarray(L0_conv_out_proj_w),
        w_cam_t=np.asarray(L1_conv_w_cam).T,
        w_q4=np.tile(np.asarray(L1_conv_w_q).T, (1, 4)), w_k4=np.tile(np.asarray(L1_conv_w_k).T, (1, 4)),
        w_v=np.asarray(L1_conv_w_v), w_bn1_t=bn[:, 0:CH].T, w_bn2_t=bn[:, CH:].T,
        consts=shape_constants())
    nc = bacc.Bacc("TRN2", target_bir_lowering=False, num_devices=1)
    given, args = {}, {}
    for name, a in arrays.items():
        a = np.ascontiguousarray(a)
        given[f"in_{name}"] = a
        args[name] = nc.dram_tensor(f"in_{name}", a.shape, mybir.dt.from_np(a.dtype), kind="ExternalInput").ap()
    out = nc.dram_tensor("out_0", (IMAGES, CH, L), F32, kind="ExternalOutput").ap()
    build(nc, out=out, **args)
    r = run_bass_kernel_spmd(nc, [given], core_ids=[0])
    return r.results[0]["out_0"].reshape(IMAGES, CH, HH, WW)
```
